# Optimizing a Trainium2 kernel written in Bass

```python
import numpy as np
import jax
import jax.numpy as jnp

def _softmax(x, axis=-1):
    return jax.nn.softmax(x, axis=axis)

def _gelu(x):
    return jax.nn.gelu(x, approximate=True)

def _silu(x):
    return jax.nn.silu(x)

def _sigmoid(x):
    return jax.nn.sigmoid(x)

def _layernorm(x, axis=-1, eps=1e-05):
    m = jnp.mean(x, axis=axis, keepdims=True)
    v = jnp.var(x, axis=axis, keepdims=True)
    return (x - m) / jnp.sqrt(v + eps)

def _scatter_add(tgt, idx, src, axis=0):
    return tgt.at[idx].add(src)

def _segment_sum(src, seg, n):
    return jax.ops.segment_sum(src, seg, n)
kernel_name = 'mk_gnn_resnorm_d2_gnn_r32_9d88b7'

def setup_inputs(seed: int=0):
    np.random.seed(seed)
    _w = jnp.asarray

    def _rec_inputs():
        import jax
        import jax.numpy as jnp
        _gk = jax.random.key(seed)
        x = -0.0003713 + 1 * jax.random.normal(jax.random.fold_in(_gk, 1), (3125, 256), jnp.float32)
        src = jax.random.randint(jax.random.fold_in(_gk, 2), (50000,), 0, 3125, jnp.int32)
        dst = jnp.minimum((3125 * jax.random.uniform(jax.random.fold_in(_gk, 3), (50000,)) ** 2.0).astype(jnp.int32), 99999)
        _o = jnp.argsort(dst, stable=True)
        src = src[_o]
        dst = dst[_o]
        edge_type_8 = jax.random.randint(jax.random.fold_in(_gk, 12), (50000,), 0, 8, jnp.int32)
        return (x, src, dst, edge_type_8)
    x, src, dst, edge_type_8 = _rec_inputs()

    def _L0_gnn_setup():
        import jax, jax.numpy as jnp
        import numpy as np
        N_NODES = 50000
        N_EDGES = 25000
        D_IN = 256
        D_HID = 256
        D_OUT = 256

        def _sage_conv(x, src, dst, Wl, bl, Wr, num_nodes):
            msg = x[src]
            agg = jax.ops.segment_sum(msg, dst, num_segments=num_nodes)
            deg = jax.ops.segment_sum(jnp.ones((src.shape[0],), x.dtype), dst, num_segments=num_nodes)
            mean = agg / jnp.maximum(deg, 1.0)[:, None]
            return jnp.einsum('nd,od->no', mean, Wl) + bl + jnp.einsum('nd,od->no', x, Wr)
        key = jax.random.key(seed)
        ks = jax.random.split(key, 12)
        x = jax.random.normal(ks[0], (N_NODES, D_IN), dtype=jnp.float32)
        edge_index = jax.random.randint(ks[1], (2, N_EDGES), 0, N_NODES, dtype=jnp.int32)

        def lin(k, dout, din):
            return jax.random.normal(k, (dout, din), dtype=jnp.float32) * (1.0 / np.sqrt(din))
        return {'x': x, 'edge_index': edge_index, 'W1l': lin(ks[2], D_HID, D_IN), 'b1l': jnp.zeros((D_HID,), jnp.float32), 'W1r': lin(ks[3], D_HID, D_IN), 'W2l': lin(ks[4], D_HID, D_HID), 'b2l': jnp.zeros((D_HID,), jnp.float32), 'W2r': lin(ks[5], D_HID, D_HID), 'W3l': lin(ks[6], D_OUT, D_HID), 'b3l': jnp.zeros((D_OUT,), jnp.float32), 'W3r': lin(ks[7], D_OUT, D_HID)}
    _L0_gnn_all = _L0_gnn_setup()
    _L0_gnn_in = {k: v for k, v in _L0_gnn_all.items() if k in ('W1l', 'b1l', 'W1r', 'W2l', 'b2l', 'W2r', 'W3l', 'b3l', 'W3r')}
    del _L0_gnn_all

    def _L1_gnn_setup():
        import jax, jax.numpy as jnp
        import numpy as np
        N_NODES = 50000
        N_EDGES = 25000
        N_REL = 8
        DIM = 256

        def _rgcn_layer(x, W, b, src, dst, edge_type, num_nodes):
            xt = jnp.einsum('ni,rio->rno', x, W)
            msg = jax.nn.relu(xt[edge_type, src] + b)
            return jax.ops.segment_sum(msg, dst, num_segments=num_nodes)
        key = jax.random.key(seed)
        ks = jax.random.split(key, 6)
        x = jax.random.normal(ks[0], (N_NODES, DIM), dtype=jnp.float32)
        limit = float(np.sqrt(6.0 / (DIM + DIM)))
        W0 = jax.random.uniform(ks[1], (N_REL, DIM, DIM), dtype=jnp.float32, minval=-limit, maxval=limit)
        W1 = jax.random.uniform(ks[2], (N_REL, DIM, DIM), dtype=jnp.float32, minval=-limit, maxval=limit)
        b0 = jnp.zeros((DIM,), dtype=jnp.float32)
        b1 = jnp.zeros((DIM,), dtype=jnp.float32)
        edge_index = jax.random.randint(ks[3], (2, N_EDGES), 0, N_NODES, dtype=jnp.int64)
        edge_type = jax.random.randint(ks[4], (N_EDGES,), 0, N_REL, dtype=jnp.int64)
        return {'x': x, 'W0': W0, 'b0': b0, 'W1': W1, 'b1': b1, 'edge_index': edge_index, 'edge_type': edge_type}
    _L1_gnn_all = _L1_gnn_setup()
    _L1_gnn_in = {k: v for k, v in _L1_gnn_all.items() if k in ('W0', 'b0', 'W1', 'b1')}
    del _L1_gnn_all
    return {'x': x, 'src': src, 'dst': dst, 'edge_type_8': edge_type_8, 'L0_gnn_W1l': _L0_gnn_in['W1l'], 'L0_gnn_b1l': _L0_gnn_in['b1l'], 'L0_gnn_W1r': _L0_gnn_in['W1r'], 'L0_gnn_W2l': _L0_gnn_in['W2l'], 'L0_gnn_b2l': _L0_gnn_in['b2l'], 'L0_gnn_W2r': _L0_gnn_in['W2r'], 'L0_gnn_W3l': _L0_gnn_in['W3l'], 'L0_gnn_b3l': _L0_gnn_in['b3l'], 'L0_gnn_W3r': _L0_gnn_in['W3r'], 'L1_gnn_W0': _L1_gnn_in['W0'], 'L1_gnn_b0': _L1_gnn_in['b0'], 'L1_gnn_W1': _L1_gnn_in['W1'], 'L1_gnn_b1': _L1_gnn_in['b1']}

def reference(x, src, dst, edge_type_8, L0_gnn_W1l, L0_gnn_b1l, L0_gnn_W1r, L0_gnn_W2l, L0_gnn_b2l, L0_gnn_W2r, L0_gnn_W3l, L0_gnn_b3l, L0_gnn_W3r, L1_gnn_W0, L1_gnn_b0, L1_gnn_W1, L1_gnn_b1):
    import jax
    import jax.numpy as jnp

    def _L0_gnn_ref(x, edge_index, W1l, b1l, W1r, W2l, b2l, W2r, W3l, b3l, W3r):
        import jax, jax.numpy as jnp
        import numpy as np
        N_NODES = 50000
        N_EDGES = 25000
        D_IN = 256
        D_HID = 256
        D_OUT = 256

        def _sage_conv(x, src, dst, Wl, bl, Wr, num_nodes):
            msg = x[src]
            agg = jax.ops.segment_sum(msg, dst, num_segments=num_nodes)
            deg = jax.ops.segment_sum(jnp.ones((src.shape[0],), x.dtype), dst, num_segments=num_nodes)
            mean = agg / jnp.maximum(deg, 1.0)[:, None]
            return jnp.einsum('nd,od->no', mean, Wl) + bl + jnp.einsum('nd,od->no', x, Wr)
        src, dst = (edge_index[0], edge_index[1])
        n = x.shape[0]
        h = _sage_conv(x, src, dst, W1l, b1l, W1r, n)
        h = jax.nn.relu(h)
        h = _sage_conv(h, src, dst, W2l, b2l, W2r, n)
        h = jax.nn.relu(h)
        h = _sage_conv(h, src, dst, W3l, b3l, W3r, n)
        return h

    def _L1_gnn_ref(x, W0, b0, W1, b1, edge_index, edge_type):
        import jax, jax.numpy as jnp
        import numpy as np
        N_NODES = 50000
        N_EDGES = 25000
        N_REL = 8
        DIM = 256

        def _rgcn_layer(x, W, b, src, dst, edge_type, num_nodes):
            xt = jnp.einsum('ni,rio->rno', x, W)
            msg = jax.nn.relu(xt[edge_type, src] + b)
            return jax.ops.segment_sum(msg, dst, num_segments=num_nodes)
        src, dst = (edge_index[0], edge_index[1])
        h = _rgcn_layer(x, W0, b0, src, dst, edge_type, x.shape[0])
        h = _rgcn_layer(h, W1, b1, src, dst, edge_type, x.shape[0])
        return h
    edge_index = jnp.stack([src, dst])
    x = _layernorm(x + _L0_gnn_ref(x, edge_index, L0_gnn_W1l, L0_gnn_b1l, L0_gnn_W1r, L0_gnn_W2l, L0_gnn_b2l, L0_gnn_W2r, L0_gnn_W3l, L0_gnn_b3l, L0_gnn_W3r), axis=-1)
    x = _layernorm(x + _L1_gnn_ref(x, L1_gnn_W0, L1_gnn_b0, L1_gnn_W1, L1_gnn_b1, edge_index, edge_type_8), axis=-1)
    return x

_drawn_inputs = setup_inputs


def setup_inputs(seed=0):
    import zlib

    import numpy as np

    out = dict(_drawn_inputs(seed))
    spreads = {'L0_gnn_b1l': (0.0, 0.28),
     'L0_gnn_b2l': (0.0, 0.1),
     'L0_gnn_b3l': (0.0, 0.1),
     'L1_gnn_b0': (0.0, 0.1),
     'L1_gnn_b1': (0.0, 0.1)}
    factors = {}
    for name, (base, spread) in spreads.items():
        noise = np.random.default_rng([zlib.crc32(name.encode()), seed]).standard_normal(out[name].shape)
        drawn = base * np.exp(spread * noise) if base else spread * noise
        out[name] = jnp.asarray(drawn.astype(out[name].dtype))
    for name, factor in factors.items():
        out[name] = (out[name] * factor).astype(out[name].dtype)
    return out
```

```python
from contextlib import ExitStack

import concourse.bass as bass
from concourse import mybir

P = 128
EPS = 1e-5


def build(nc, x, src, dst, edge_type, sage_w, sage_b, rel_w, rel_b, out, n_edges, n_rel):
    fp32, i32, u32 = mybir.dt.float32, mybir.dt.int32, mybir.dt.uint32
    bf16, u16 = mybir.dt.bfloat16, mybir.dt.uint16
    ALU, ACT, AX = mybir.AluOpType, mybir.ActivationFunctionType, mybir.AxisListType

    n_pad, D = x.shape
    TILES = n_pad // P
    CHUNKS = src.shape[0] // P
    DK = D // P
    CG = -(-CHUNKS // P)
    LAST = CHUNKS - (CG - 1) * P
    BLOCK = 512
    MAX_STEPS = CHUNKS * TILES
    MAX_BLOCKS = -(-MAX_STEPS // BLOCK)
    CAP = MAX_BLOCKS * BLOCK
    G = 8
    HALF = G // 2
    MAX_GROUPS = -(-MAX_STEPS // G)
    PACK, BITS = 4, 5
    assert TILES <= 1 << BITS and PACK * BITS <= 24
    U = 5
    assert TILES % U == 0
    ITER = TILES // U
    SAGE = len(sage_w)
    LAYERS = SAGE + len(rel_w)
    QR = 2
    QN = n_rel // QR
    RH = n_rel // 2
    DW = D + 1

    ctx = ExitStack()
    with ctx:
        def sb(name, shape, dt):
            return ctx.enter_context(nc.sbuf_tensor(name, shape, dt))

        def sem(name):
            return ctx.enter_context(nc.semaphore(name))

        h_dram = [nc.dram_tensor(f"h{n}_rows", (n_pad, D), fp32).ap() for n in range(SAGE - 1)]
        x1_dram = nc.dram_tensor("x1_rows", (n_pad, D), fp32).ap()
        rel_dram = [nc.dram_tensor(f"rel{n}_rows", (n_rel, n_pad, D), fp32).ap() for n in range(LAYERS - SAGE)]
        sources = [x, *h_dram] + [r.rearrange("r n d -> (r n) d") for r in rel_dram]

        acc = sb("acc", [P, TILES, DW], fp32)
        right = sb("right", [P, TILES, D], fp32)
        src_steps = sb("src_steps", [P, CAP], u16)
        rel_steps = sb("rel_steps", [P, CAP], u16)
        dst_steps = sb("dst_steps", [P, CAP], bf16)
        tile_words = sb("tile_words", [1, CAP // PACK], i32)
        ring = sb("ring", [P, G, DW], fp32)
        onehot = sb("onehot", [P, G, P], fp32)
        idx = sb("idx", [P, G], u32)
        w_sage = sb("w_sage", [P, SAGE, 2, DK, D], fp32)
        bias_sage = sb("bias_sage", [P, SAGE, D], fp32)
        bias_rel = sb("bias_rel", [P, LAYERS - SAGE, D], fp32)
        ident = sb("ident", [P, P], fp32)
        ones = sb("ones", [P, P], fp32)
        before = sb("before", [P, P], fp32)
        iota = sb("iota", [P, BLOCK], fp32)
        zeros = sb("zeros", [P, DW], fp32)
        rdeg = sb("rdeg", [P, TILES], fp32)
        counts = sb("counts", [1, 2], i32)
        small = sb("small", [P, 64], fp32)
        small_i = sb("small_i", [P, 2 * CG + 2], i32)
        stats = sb("stats", [P, U, 6], fp32)
        mv = sb("mv", [P, U, 2], fp32)
        rstd = sb("rstd", [P, U], fp32)
        late = sb("late", [P, (DK + 1) * n_rel * D], fp32)
        w_rel = late[:, 0:DK * n_rel * D].rearrange("p (k r d) -> p k r d", k=DK, r=n_rel)
        rel_out = late[:, DK * n_rel * D:(DK + 1) * n_rel * D].rearrange("p (h r d) -> p h r d", h=2, r=RH)
        rows = late[:, 0:4 * CG * P].rearrange("p (k g e) -> p k g e", k=4, g=CG)
        select = late[:, 4 * CG * P:8 * CG * P].rearrange("p (g s) -> p g s", g=CG)
        raw = late[:, 8 * CG * P:11 * CG * P].bitcast(i32).rearrange("p (k g e) -> p k g e", k=3, g=CG)
        assert BLOCK == CG * P and 11 * CG * P <= (DK + 1) * n_rel * D
        entry = sb("entry", [P, U, D], fp32)
        meanT = sb("meanT", [P, U, D], fp32)
        h_new = sb("h_new", [P, U, D], fp32)
        x_res = sb("x_res", [P, U, D], fp32)
        turned = sb("turned", [P, U, D], fp32)
        tile_row = onehot[:, 0:BLOCK // P, :].rearrange("p a b -> p (a b)")
        step_row = onehot[:, BLOCK // P:2 * BLOCK // P, :].rearrange("p a b -> p (a b)")

        ps = ctx.enter_context(nc.psum_tensor("ps", [P, 8, 512], fp32))
        ps_meanT = ps_y = ps_turned = ps_right = ps[:, 0:U, 0:D]
        rel_bank = [*range(U, 8), 0][:QN]
        ps_scan = ps[:, 5, 0:2 * CG]

        first_tile, tiles_of, start, end, base_less, totals = (
            small[:, n * CG:(n + 1) * CG] for n in range(6))
        total, block_base, least, most = small[:, 6 * CG:6 * CG + 1], small[:, 6 * CG + 1:6 * CG + 2], \
            small[:, 7 * CG:8 * CG], small[:, 8 * CG:9 * CG]
        in_use = small[:, 9 * CG:10 * CG]

        raw_cleared = sem("raw_cleared")
        edges_loaded = sem("edges_loaded")
        sage_w_loaded, bias_loaded = sem("sage_w_loaded"), sem("bias_loaded")
        rel_w_loaded = [sem(f"rel_w_loaded{n}") for n in range(LAYERS - SAGE)]
        dve_link = sem("dve_link")
        constants = sem("constants")
        dst_ready, dst_masked = sem("dst_ready"), sem("dst_masked")
        spans_ready, scanned = sem("spans_ready"), sem("scanned")
        counts_ready = sem("counts_ready")
        selected, listed = sem("selected"), sem("listed")
        block_link = sem("block_link")
        idx_ready = [sem(f"idx_ready{n}") for n in range(LAYERS)]
        landed = [[sem(f"landed{n}_{j}") for j in range(G)] for n in range(LAYERS)]
        onehot_ready = [sem(f"onehot_ready{n}") for n in range(LAYERS)]
        summed = [sem(f"summed{n}") for n in range(LAYERS)]
        accumulated = [sem(f"accumulated{n}") for n in range(LAYERS)]
        cleared = sem("cleared")
        deg_ready = sem("deg_ready")
        averaged, mean_turned, mean_kept = sem("averaged"), sem("mean_turned"), sem("mean_kept")
        y_ready, biased, h_ready = sem("y_ready"), sem("biased"), sem("h_ready")
        h_stored = [sem(f"h_stored_{u}") for u in range(U)]
        x_loaded = [sem(f"x_loaded_{u}") for u in range(U)]
        copied = sem("copied")
        tile_turned, tile_kept = sem("tile_turned"), sem("tile_kept")
        right_ready, right_kept = sem("right_ready"), sem("right_kept")
        rel_ready = sem("rel_ready")
        rel_biased = sem("rel_biased")
        rel_relu = sem("rel_relu")
        rel_stored = [sem(f"rel_stored_{h}") for h in range(2)]
        res_loaded = [sem(f"res_loaded_{u}") for u in range(U)]
        var_ready = [sem(f"var_ready{n}") for n in range(2)]
        std_ready = [sem(f"std_ready{n}") for n in range(2)]
        norm_link = [sem(f"norm_link{n}") for n in range(2)]
        normed = sem("normed")
        slots_freed, stats_taken = sem("slots_freed"), sem("stats_taken")
        res_added, last_added = sem("res_added"), sem("last_added")
        out_stored = [sem(f"out_stored{u}") for u in range(U)]

        block = ctx.enter_context(nc.Block())

        def node_rows(dram, t):
            return dram[bass.ds(t * P, P), :]

        def load_groups(eng):
            eng.wait_ge(counts_ready, 1)
            return eng.value_load(counts[0:1, 0:1], min_val=2, max_val=MAX_GROUPS)

        def load_blocks(eng):
            eng.wait_ge(counts_ready, 1)
            return eng.value_load(counts[0:1, 1:2], min_val=1, max_val=MAX_BLOCKS)

        def peeled(eng, n, body):
            body(0, True)
            with eng.Fori(1, n) as i:
                body(i, False)

        @block.sync
        def _(sp):
            sp.wait_ge(raw_cleared, 1)
            for k, e in enumerate((dst, src, edge_type)):
                full = (CG - 1) * P * P
                sp.dma_start(raw[:, k, 0:CG - 1, :],
                             e[0:full].rearrange("(g p e) -> p g e", g=CG - 1, p=P)).then_inc(edges_loaded, 16)
                sp.dma_start(raw[0:LAST, k, CG - 1, :],
                             e[full:full + LAST * P].rearrange("(p e) -> p e", p=LAST)).then_inc(edges_loaded, 16)
            for n, ws in enumerate(sage_w):
                for m, w in enumerate(ws):
                    sp.dma_start(w_sage[:, n, m, :, :],
                                 w.rearrange("(k p) o -> p k o", p=P)).then_inc(sage_w_loaded, 16)
            for n, b in enumerate(sage_b):
                sp.dma_start(bias_sage[:, n, :], b.partition_broadcast(P)).then_inc(bias_loaded, 16)
            for n, b in enumerate(rel_b):
                sp.dma_start(bias_rel[:, n, :], b.partition_broadcast(P)).then_inc(bias_loaded, 16)

            def load_rel_w(n):
                for k in range(DK):
                    sp.dma_start(w_rel[:, k, :, :],
                                 rel_w[n][:, k * P:(k + 1) * P, :].rearrange("r p o -> p r o")).then_inc(rel_w_loaded[n], 16)

            def load_x(i, first):
                for u in range(U):
                    if not first:
                        sp.wait_ge(tile_turned, (i - 1) * U + u + 1)
                    sp.dma_start(entry[:, u, :], node_rows(x, i * U + u)).then_inc(x_loaded[u], 16)
            peeled(sp, ITER, load_x)
            sp.wait_ge(counts_ready, 2)
            load_rel_w(0)

            def store_rels(n, i):
                for u in range(U):
                    t = i * U + u
                    for h in range(2):
                        sp.wait_ge(rel_relu, (n * TILES + t) * QN + (h + 1) * QN // 2)
                        sp.dma_start(rel_dram[n][RH * h:RH * (h + 1), bass.ds(t * P, P), :].rearrange("r p d -> p r d"),
                                     rel_out[:, h, :, :]).then_inc(rel_stored[h], 16)

            for n in range(SAGE):
                target = h_dram[n] if n < SAGE - 1 else x1_dram

                def store(i, first, n=n, target=target):
                    for u in range(U):
                        if n == SAGE - 1:
                            if not first:
                                sp.wait_ge(h_ready, n * TILES + (i - 1) * U + u + 1)
                            sp.dma_start(x_res[:, u, :], node_rows(x, i * U + u)).then_inc(res_loaded[u], 16)
                    for u in range(U):
                        sp.wait_ge(h_ready, n * TILES + i * U + u + 1)
                        sp.dma_start(node_rows(target, i * U + u), h_new[:, u, :]).then_inc(h_stored[u], 16)
                    if n == SAGE - 1:
                        store_rels(0, i)
                peeled(sp, ITER, store)

            for n in range(1, LAYERS - SAGE):
                sp.wait_ge(rel_ready, n * QN * TILES)
                load_rel_w(n)
                with sp.Fori(0, ITER) as i:
                    store_rels(n, i)

            for u in range(U):
                sp.wait_ge(h_stored[u], 16 * ITER * SAGE)

            def last(i, first):
                for u in range(U):
                    if not first:
                        sp.wait_ge(normed, (i - 1) * U + u + 1)
                    sp.dma_start(x_res[:, u, :], node_rows(x1_dram, i * U + u)).then_inc(res_loaded[u], 16)
                for u in range(U):
                    sp.wait_ge(normed, i * U + u + 1)
                    sp.dma_start(node_rows(out, i * U + u), h_new[:, u, :]).then_inc(out_stored[u], 16)
            peeled(sp, ITER, last)
            for u in range(U):
                sp.wait_ge(out_stored[u], 16 * ITER)

        @block.gpsimd
        def _(pool):
            pool.memset(raw[:, :, CG - 1, :], 0).then_inc(raw_cleared, 1)
            pool.iota(iota[:, :], pattern=[[1, BLOCK]], base=0, channel_multiplier=0,
                      allow_small_or_imprecise_dtypes=True).then_inc(constants, 1)
            pool.memset(ones[:, :], 1.0).then_inc(constants, 1)
            pool.memset(zeros[:, :], 0.0).then_inc(constants, 1)
            pool.memset(ring[:, :, D:DW], 1.0).then_inc(constants, 1)
            pool.memset(acc[:, :, :], 0.0).then_inc(cleared, 1)
            pool.wait_ge(constants, 3)
            pool.affine_select(out=ident[:, :], in_=zeros[:, 0:P], compare_op=ALU.not_equal, fill=1.0,
                               base=0, pattern=[[-1, P]], channel_multiplier=1).then_inc(constants, 1)
            pool.affine_select(out=before[:, :], in_=ones[:, :], compare_op=ALU.is_gt, fill=0.0,
                               base=0, pattern=[[1, P]], channel_multiplier=-1).then_inc(constants, 1)
            pool.affine_select(out=in_use, in_=ones[:, 0:CG], compare_op=ALU.is_ge, fill=0.0,
                               base=CHUNKS - 1, pattern=[[-P, CG]], channel_multiplier=-1).then_inc(constants, 1)
            pool.wait_ge(dst_ready, 1)
            pool.affine_select(out=rows[:, 0, :, :], in_=rows[:, 0, :, :], compare_op=ALU.is_ge,
                               fill=-float(1 << 14), base=n_edges - 1, pattern=[[-P * P, CG], [-1, P]],
                               channel_multiplier=-P).then_inc(dst_masked, 1)

            def clear_tiles(gate, base):
                with pool.Fori(0, TILES) as t:
                    pool.wait_ge(gate, base + t + 1)
                    pool.tensor_copy(acc[:, bass.ds(t, 1), :].rearrange("p a d -> p (a d)"),
                                     zeros[:, :]).then_inc(cleared, 1)

            def gathers(n):
                def group(g, first):
                    for j in range(G):
                        if j % HALF == 0:
                            pool.wait_ge(idx_ready[n], 2 * g + j // HALF + 1)
                        if not first:
                            pool.wait_ge(summed[n], (g - 1) * G + j + 1)
                            pool.sem_inc(slots_freed, 1)
                        pool.indirect_dma_start(
                            out=ring[:, j, 0:D], out_offset=None, in_=sources[n],
                            in_offset=bass.IndirectOffsetOnAxis(ap=idx[:, j:j + 1], axis=0),
                        ).then_inc(landed[n][j], 16)
                peeled(pool, groups, group)

            groups = load_groups(pool)
            for n in range(LAYERS):
                if 0 < n < SAGE:
                    for u in range(U):
                        pool.wait_ge(h_stored[u], 16 * ITER * n)
                elif n >= SAGE:
                    for h in range(2):
                        pool.wait_ge(rel_stored[h], 16 * TILES * (n + 1 - SAGE))
                gathers(n)
                if n < SAGE:
                    clear_tiles(averaged, n * TILES)
                elif n < LAYERS - 1:
                    clear_tiles(copied, 0)

        @block.scalar
        def _(act):
            def keep_turned(p, i, first):
                for u in range(U):
                    t = p * TILES + i * U + u
                    act.wait_ge(tile_turned, t + 1)
                    if p <= SAGE - 1:
                        if p > 0 or not first:
                            act.wait_ge(right_ready, t - U + 1)
                    elif p > SAGE or not first:
                        act.wait_ge(rel_ready, QN * (t - SAGE * TILES - U + 1))
                    act.activation(turned[:, u, :], ps_turned[:, u, :], ACT.Copy).then_inc(tile_kept, 1)

            def indices(n):
                steps = src_steps if n < SAGE else rel_steps

                def group(g, first):
                    for h in range(2):
                        if not first:
                            act.wait_ge(summed[n], (g - 1) * G + (h + 1) * HALF)
                        act.activation(idx[:, h * HALF:(h + 1) * HALF],
                                       steps[:, bass.ds(g * G + h * HALF, HALF)],
                                       ACT.Copy).then_inc(idx_ready[n], 1)
                peeled(act, groups, group)

            def sage_tail(n):
                act.wait_ge(accumulated[n], groups * G)
                if n == 0:
                    act.wait_ge(deg_ready, 1)

                def body(i, first):
                    for u in range(U):
                        t = i * U + u
                        if not first:
                            act.wait_ge(mean_turned, n * TILES + t - U + 1)
                        act.activation(entry[:, u, :], acc[:, bass.ds(t, 1), 0:D].rearrange("p a d -> p (a d)"),
                                       ACT.Copy, scale=rdeg[:, bass.ds(t, 1)]).then_inc(averaged, 1)
                    if n < SAGE - 1:
                        for u in range(U):
                            act.wait_ge(biased, n * TILES + i * U + u + 1)
                            act.activation(h_new[:, u, :], h_new[:, u, :], ACT.Relu).then_inc(h_ready, 1)
                    else:
                        act.wait_ge(var_ready[0], i + 1)
                        act.activation(rstd[:, :], rstd[:, :], ACT.Sqrt).then_inc(std_ready[0], 1)
                    keep_turned(n + 1, i, first)
                    if n == SAGE - 1:
                        rel_relus(0, i)
                peeled(act, ITER, body)

            def rel_relus(n, i):
                for u in range(U):
                    t = n * TILES + i * U + u
                    for q in range(QN):
                        act.wait_ge(rel_biased, t * QN + q + 1)
                        part = rel_out[:, q * QR // RH, q * QR % RH:q * QR % RH + QR, :]
                        act.activation(part, part, ACT.Relu).then_inc(rel_relu, 1)

            def second_table():
                act.wait_ge(accumulated[SAGE], groups * G)

                def body(i, first):
                    for u in range(U):
                        t = i * U + u
                        if not first:
                            act.wait_ge(tile_turned, (SAGE + 1) * TILES + t - U + 1)
                        act.activation(entry[:, u, :], acc[:, bass.ds(t, 1), 0:D].rearrange("p a d -> p (a d)"),
                                       ACT.Copy).then_inc(copied, 1)
                    keep_turned(SAGE + 1, i, first)
                    rel_relus(1, i)
                peeled(act, ITER, body)

            peeled(act, ITER, lambda i, first: keep_turned(0, i, first))
            groups = load_groups(act)
            act.wait_ge(counts_ready, 2)
            for n in range(LAYERS):
                indices(n)
                if n < SAGE:
                    sage_tail(n)
                elif n == SAGE:
                    second_table()
            with act.Fori(0, ITER) as i:
                act.wait_ge(var_ready[1], i + 1)
                act.activation(rstd[:, :], rstd[:, :], ACT.Sqrt).then_inc(std_ready[1], 1)

        @block.tensor
        def _(pe):
            def turn(slots, target, u):
                for d in range(DK):
                    last = pe.transpose(target[:, u, d * P:(d + 1) * P], slots[:, u, d * P:(d + 1) * P], ident[:, :])
                return last

            def multiply(target, slots, u, w):
                for d in range(DK):
                    last = pe.matmul(target, slots[:, u, d * P:(d + 1) * P], w[d], start=(d == 0), stop=(d == DK - 1))
                return last

            def rights(p, i):
                for u in range(U):
                    t = p * TILES + i * U + u
                    pe.wait_ge(tile_kept, t + 1)
                    multiply(ps_right[:, u, :], turned, u,
                             [w_sage[:, p, 1, d, :] for d in range(DK)]).then_inc(right_ready, 1)

            def rel_products(n, i, first):
                for u in range(U):
                    t = i * U + u
                    pe.wait_ge(tile_kept, (SAGE + n) * TILES + t + 1)
                    for q in range(QN):
                        if not first or u > 0:
                            pe.wait_ge(rel_biased, (n * TILES + t - 1) * QN + q + 1)
                        multiply(ps[:, rel_bank[q], :], turned, u,
                                 [w_rel[:, d, q * QR:(q + 1) * QR, :].rearrange("p r o -> p (r o)")
                                  for d in range(DK)]).then_inc(rel_ready, 1)

            def sums(n):
                def group(g, first):
                    pe.wait_ge(onehot_ready[n], g + 1)
                    for j in range(G):
                        if not first:
                            pe.wait_ge(accumulated[n], (g - 1) * G + j + 1)
                        pe.wait_ge(landed[n][j], 16 * (g + 1))
                        pe.matmul(ps[:, j, 0:DW], onehot[:, j, :], ring[:, j, :],
                                  start=True, stop=True).then_inc(summed[n], 1)
                peeled(pe, groups, group)

            def sage_tail(n):
                pe.wait_ge(accumulated[n], groups * G)

                def body(i, first):
                    for u in range(U):
                        t = i * U + u
                        pe.wait_ge(averaged, n * TILES + t + 1)
                        if not first:
                            if n < SAGE - 1:
                                pe.wait_ge(right_kept, (n + 1) * TILES + t - U + 1)
                            elif u in rel_bank:
                                pe.wait_ge(rel_biased, i * U * QN)
                        turn(entry, ps_meanT, u).then_inc(mean_turned, 1)
                    for u in range(U):
                        t = i * U + u
                        pe.wait_ge(mean_kept, n * TILES + t + 1)
                        multiply(ps_y[:, u, :], meanT, u,
                                 [w_sage[:, n, 0, d, :] for d in range(DK)]).then_inc(y_ready, 1)
                    for u in range(U):
                        t = i * U + u
                        pe.wait_ge(h_ready, n * TILES + t + 1)
                        turn(h_new, ps_turned, u).then_inc(tile_turned, 1)
                    if n < SAGE - 1:
                        rights(n + 1, i)
                    else:
                        rel_products(0, i, first)
                peeled(pe, ITER, body)

            def second_table():
                pe.wait_ge(accumulated[SAGE], groups * G)
                pe.wait_ge(rel_w_loaded[1], 16 * DK)

                def body(i, first):
                    for u in range(U):
                        t = i * U + u
                        pe.wait_ge(copied, t + 1)
                        if not first and u in rel_bank:
                            pe.wait_ge(rel_biased, (TILES + i * U) * QN)
                        turn(entry, ps_turned, u).then_inc(tile_turned, 1)
                    rel_products(1, i, first)
                peeled(pe, ITER, body)

            pe.wait_ge(constants, 7)
            pe.wait_ge(spans_ready, 1)
            pe.matmul(ps_scan[:, 0:CG], before[:, :], tiles_of, start=True, stop=True)
            pe.matmul(ps_scan[:, CG:2 * CG], ones[:, :], tiles_of, start=True, stop=True).then_inc(scanned, 1)
            blocks = load_blocks(pe)

            with pe.Fori(0, blocks) as b:
                pe.wait_ge(selected, b + 1)
                for k in range(4):
                    for g in range(CG):
                        last = pe.matmul(ps[:, k, :], rows[:, k, g, :], select[:, g, :],
                                         start=(g == 0), stop=(g == CG - 1))
                last.then_inc(listed, 1)

            pe.wait_ge(sage_w_loaded, 16 * 2 * SAGE)
            pe.wait_ge(counts_ready, 2)

            def x_pass(i, first):
                for u in range(U):
                    t = i * U + u
                    pe.wait_ge(x_loaded[u], 16 * (i + 1))
                    if not first:
                        pe.wait_ge(right_kept, t - U + 1)
                    turn(entry, ps_turned, u).then_inc(tile_turned, 1)
                rights(0, i)
            peeled(pe, ITER, x_pass)

            groups = load_groups(pe)
            for n in range(LAYERS):
                if n <= SAGE - 1:
                    pe.wait_ge(right_kept, (n + 1) * TILES)
                else:
                    pe.wait_ge(rel_biased, (n + 1 - SAGE) * QN * TILES)
                sums(n)
                if n == SAGE - 1:
                    pe.wait_ge(rel_w_loaded[0], 16 * DK)
                if n < SAGE:
                    sage_tail(n)
                elif n == SAGE:
                    second_table()

        @block.vector
        def _(dve):
            linked = [0]

            def link(ins):
                linked[0] += 1
                ins.then_inc(dve_link, 1)
                dve.wait_ge(dve_link, linked[0])

            dve.wait_ge(edges_loaded, 16 * 6)
            dve.tensor_copy(rows[:, 0, :, :], raw[:, 0, :, :]).then_inc(dst_ready, 1)
            dve.tensor_copy(rows[:, 1, :, :], raw[:, 1, :, :])
            link(dve.tensor_reduce(least, raw[:, 0, :, :], axis=AX.X, op=ALU.min))
            link(dve.tensor_reduce(most, raw[:, 0, :, :], axis=AX.X, op=ALU.max))
            link(dve.scalar_tensor_tensor(rows[:, 2, :, :], raw[:, 2, :, :], float(n_pad), rows[:, 1, :, :],
                                          op0=ALU.mult, op1=ALU.add))
            link(dve.tensor_copy(small_i[:, 0:2 * CG], small[:, 7 * CG:9 * CG]))
            link(dve.tensor_scalar(small_i[:, 0:2 * CG], small_i[:, 0:2 * CG], 7, None, op0=ALU.arith_shift_right))
            link(dve.tensor_copy(small[:, 7 * CG:9 * CG], small_i[:, 0:2 * CG]))
            link(dve.tensor_copy(first_tile, least))
            dve.wait_ge(constants, 7)
            link(dve.tensor_tensor(tiles_of, most, least, op=ALU.subtract))
            link(dve.tensor_scalar(tiles_of, tiles_of, 1.0, None, op0=ALU.add))
            link(dve.tensor_tensor(tiles_of, tiles_of, in_use, op=ALU.mult))
            dve.sem_inc(spans_ready, 1)
            dve.wait_ge(scanned, 1)
            link(dve.tensor_copy(totals, ps_scan[:, CG:2 * CG]))
            link(dve.tensor_copy(start, ps_scan[:, 0:CG]))
            for g in range(1, CG):
                for before_g in range(g):
                    link(dve.tensor_tensor(start[:, g:g + 1], start[:, g:g + 1], totals[:, before_g:before_g + 1],
                                           op=ALU.add))
            link(dve.tensor_tensor(end, start, tiles_of, op=ALU.add))
            link(dve.tensor_tensor(base_less, first_tile, start, op=ALU.subtract))
            link(dve.tensor_reduce(total, totals, axis=AX.X, op=ALU.add))
            for n, width in enumerate((G, BLOCK)):
                link(dve.tensor_scalar(small_i[:, 2 * CG + n:2 * CG + n + 1], total, float(width - 1), None, op0=ALU.add))
                link(dve.tensor_scalar(counts[0:1, n:n + 1], small_i[0:1, 2 * CG + n:2 * CG + n + 1],
                                       width.bit_length() - 1, None, op0=ALU.arith_shift_right))
            dve.sem_inc(counts_ready, 1)
            for g in range(CG):
                link(dve.tensor_scalar(rows[:, 3, g, :], ones[:, :], base_less[:, g:g + 1], None, op0=ALU.mult))
            link(dve.memset(block_base, 0.0))
            blocks = load_blocks(dve)
            dve.wait_ge(dst_masked, 1)
            LINKS = 2 * CG + 2 + 1 + (PACK - 1) + 3 + 3

            def list_block(b):
                at = [0]

                def chain(ins):
                    at[0] += 1
                    ins.then_inc(block_link, 1)
                    dve.wait_ge(block_link, b * LINKS + at[0])
                for g in range(CG):
                    chain(dve.tensor_scalar(tile_row, iota[:, :], start[:, g:g + 1], None, op0=ALU.is_ge))
                    chain(dve.scalar_tensor_tensor(select[:, g, :], iota[:, :], end[:, g:g + 1], tile_row,
                                                   op0=ALU.is_lt, op1=ALU.mult))
                dve.sem_inc(selected, 1)
                dve.wait_ge(listed, b + 1)
                chain(dve.scalar_tensor_tensor(tile_row, iota[:, :], block_base, ps[:, 3, :],
                                               op0=ALU.add, op1=ALU.add))
                chain(dve.tensor_scalar(tile_row, tile_row, float(TILES - 1), None, op0=ALU.min))
                chain(dve.scalar_tensor_tensor(dst_steps[:, bass.ds(b * BLOCK, BLOCK)], tile_row, -float(P),
                                               ps[:, 0, :], op0=ALU.mult, op1=ALU.add))
                quads = tile_row[0:1, :].rearrange("p (s k) -> p k s", k=PACK)
                words = step_row[0:1, 0:BLOCK // PACK]
                word = quads[:, PACK - 1, :]
                for k in reversed(range(PACK - 1)):
                    chain(dve.scalar_tensor_tensor(words, word, float(1 << BITS), quads[:, k, :],
                                                   op0=ALU.mult, op1=ALU.add))
                    word = words
                chain(dve.tensor_copy(tile_words[0:1, bass.ds(b * (BLOCK // PACK), BLOCK // PACK)], words))
                chain(dve.tensor_copy(src_steps[:, bass.ds(b * BLOCK, BLOCK)], ps[:, 1, :]))
                chain(dve.tensor_copy(rel_steps[:, bass.ds(b * BLOCK, BLOCK)], ps[:, 2, :]))
                chain(dve.tensor_scalar(start, start, -float(BLOCK), None, op0=ALU.add))
                chain(dve.tensor_scalar(end, end, -float(BLOCK), None, op0=ALU.add))
                chain(dve.tensor_scalar(block_base, block_base, float(BLOCK), None, op0=ALU.add))
                assert at[0] == LINKS
            with dve.Fori(0, blocks) as b:
                list_block(b)
            dve.sem_inc(counts_ready, 1)
            groups = load_groups(dve)

            def sums(n):
                def group(g, first):
                    if not first:
                        dve.wait_ge(summed[n], g * G)
                    dve.tensor_tensor(
                        onehot[:, :, :],
                        iota[:, 0:P].rearrange("p (a d) -> p a d", a=1).to_broadcast([P, G, P]),
                        dst_steps[:, bass.ds(g * G, G)].rearrange("p (g a) -> p g a", a=1).to_broadcast([P, G, P]),
                        op=ALU.is_equal).then_inc(onehot_ready[n], 1)
                    words = [dve.value_load(tile_words[0:1, bass.ds(g * (G // PACK) + w, 1)], min_val=0,
                                            max_val=(1 << BITS * PACK) - 1) for w in range(G // PACK)]
                    for j in range(G):
                        t = nc.s_assert_within((words[j // PACK] >> (BITS * (j % PACK))) & ((1 << BITS) - 1),
                                               0, TILES - 1,
                                               skip_runtime_bounds_check_because="the list holds numbers of tiles only")
                        dve.wait_ge(summed[n], g * G + j + 1)
                        if not (first and j == 0):
                            dve.wait_ge(accumulated[n], g * G + j)
                        tile = acc[:, bass.ds(t, 1), :].rearrange("p a d -> p (a d)")
                        dve.tensor_tensor(tile, tile, ps[:, j, 0:DW], op=ALU.add).then_inc(accumulated[n], 1)
                dve.wait_ge(cleared, n * TILES + 1)
                peeled(dve, groups, group)
                dve.wait_ge(accumulated[n], groups * G)

            NORM_LINKS = 2 * U + 2

            def norm(m, i, ready):
                at = [0]

                def chain(ins):
                    at[0] += 1
                    ins.then_inc(norm_link[m], 1)
                    dve.wait_ge(norm_link[m], i * NORM_LINKS + at[0])
                for u in range(U):
                    chain(dve.bn_stats(stats[:, u, :], h_new[:, u, :]))
                dve.sem_inc(stats_taken, 1)
                for u in range(U):
                    at[0] += 1
                    dve.bn_aggr(mv[:, u, :], stats[:, u, :]).then_inc(norm_link[m], 1)
                dve.wait_ge(norm_link[m], i * NORM_LINKS + at[0])
                dve.tensor_scalar(rstd[:, :], mv[:, :, 1], EPS, None, op0=ALU.add).then_inc(var_ready[m], 1)
                dve.wait_ge(std_ready[m], i + 1)
                chain(dve.reciprocal(rstd[:, :], rstd[:, :]))
                chain(dve.tensor_copy(mv[:, :, 1], rstd[:, :]))
                assert at[0] == NORM_LINKS
                for u in range(U):
                    dve.tensor_scalar(h_new[:, u, :], h_new[:, u, :], mv[:, u, 0:1], rstd[:, u:u + 1],
                                      op0=ALU.subtract, op1=ALU.mult).then_inc(ready, 1)

            def keep_rights(p, i):
                for u in range(U):
                    t = i * U + u
                    dve.wait_ge(right_ready, p * TILES + t + 1)
                    dve.tensor_tensor(right[:, bass.ds(t, 1), :].rearrange("p a d -> p (a d)"), ps_right[:, u, :],
                                      bias_sage[:, p, :], op=ALU.add).then_inc(right_kept, 1)

            def rel_biases(n, i, first):
                for u in range(U):
                    t = n * TILES + i * U + u
                    for q in range(QN):
                        dve.wait_ge(rel_ready, t * QN + q + 1)
                        if q % (QN // 2) == 0 and (n > 0 or not first or u > 0):
                            dve.wait_ge(rel_stored[2 * q // QN], 16 * t)
                        part = rel_out[:, q * QR // RH, q * QR % RH:q * QR % RH + QR, :]
                        dve.tensor_tensor(part, ps[:, rel_bank[q], :].rearrange("p (r d) -> p r d", r=QR),
                                          bias_rel[:, n:n + 1, :].to_broadcast([P, QR, D]),
                                          op=ALU.add).then_inc(rel_biased, 1)

            def sage_tail(n):
                def body(i, first):
                    for u in range(U):
                        t = n * TILES + i * U + u
                        dve.wait_ge(mean_turned, t + 1)
                        if not first:
                            dve.wait_ge(y_ready, t - U + 1)
                        dve.tensor_copy(meanT[:, u, :], ps_meanT[:, u, :]).then_inc(mean_kept, 1)
                    for u in range(U):
                        t = i * U + u
                        dve.wait_ge(y_ready, n * TILES + t + 1)
                        if n > 0 or not first:
                            dve.wait_ge(tile_turned, (n + 1) * TILES + t - U + 1)
                            dve.wait_ge(h_stored[u], 16 * (n * ITER + i))
                        dve.tensor_tensor(h_new[:, u, :], ps_y[:, u, :],
                                          right[:, bass.ds(t, 1), :].rearrange("p a d -> p (a d)"),
                                          op=ALU.add).then_inc(biased, 1)
                        if n == SAGE - 1:
                            dve.wait_ge(biased, n * TILES + t + 1)
                            dve.wait_ge(res_loaded[u], 16 * (i + 1))
                            dve.tensor_tensor(h_new[:, u, :], h_new[:, u, :], x_res[:, u, :],
                                              op=ALU.add).then_inc(res_added, 1)
                    if n < SAGE - 1:
                        keep_rights(n + 1, i)
                    else:
                        dve.wait_ge(res_added, (i + 1) * U)
                        norm(0, i, h_ready)
                        rel_biases(0, i, first)
                peeled(dve, ITER, body)

            dve.wait_ge(bias_loaded, 16 * LAYERS)
            with dve.Fori(0, ITER) as i:
                keep_rights(0, i)
            for n in range(LAYERS):
                sums(n)
                if n == 0:
                    link(dve.tensor_scalar(rdeg[:, :], acc[:, :, D], 1.0, None, op0=ALU.max))
                    link(dve.reciprocal(rdeg[:, :], rdeg[:, :]))
                    dve.sem_inc(deg_ready, 1)
                if n < SAGE:
                    sage_tail(n)
                elif n == SAGE:
                    peeled(dve, ITER, lambda i, first: rel_biases(1, i, first))

            def last(i, first):
                for u in range(U):
                    dve.wait_ge(res_loaded[u], 16 * (ITER + i + 1))
                    if not first:
                        dve.wait_ge(out_stored[u], 16 * i)
                    dve.tensor_tensor(h_new[:, u, :], x_res[:, u, :],
                                      acc[:, bass.ds(i * U + u, 1), 0:D].rearrange("p a d -> p (a d)"),
                                      op=ALU.add).then_inc(last_added, 1)
                dve.wait_ge(last_added, (i + 1) * U)
                norm(1, i, normed)
            for u in range(U):
                dve.wait_ge(h_stored[u], 16 * ITER * SAGE)
            peeled(dve, ITER, last)


def kernel(**inputs):
    import numpy as np
    import concourse.bacc as bacc
    from concourse.bass_utils import run_bass_kernel_spmd

    x = np.asarray(inputs["x"])
    n_nodes, d = x.shape
    n_edges = inputs["src"].shape[0]
    w_rel = [np.ascontiguousarray(inputs[f"L1_gnn_W{n}"]) for n in range(2)]
    n_rel = w_rel[0].shape[0]
    arrays = {
        "x": np.pad(x, ((0, -n_nodes % P), (0, 0))),
        **{k: np.pad(np.asarray(inputs[k]), (0, -n_edges % P), mode="edge") for k in ("src", "dst", "edge_type_8")},
        **{f"W{n}{s}": np.ascontiguousarray(np.asarray(inputs[f"L0_gnn_W{n}{s}"]).T) for n in (1, 2, 3) for s in "lr"},
        **{f"b{n}": np.asarray(inputs[f"L0_gnn_b{n}l"]) for n in (1, 2, 3)},
        **{f"Wrel{n}": w_rel[n] for n in range(2)},
        **{f"brel{n}": np.asarray(inputs[f"L1_gnn_b{n}"]) for n in range(2)},
    }
    nc = bacc.Bacc("TRN2", target_bir_lowering=False, num_devices=1)
    t = {k: nc.dram_tensor(f"in_{k}", a.shape, mybir.dt.from_np(a.dtype), kind="ExternalInput").ap()
         for k, a in arrays.items()}
    out = nc.dram_tensor("out", arrays["x"].shape, mybir.dt.float32, kind="ExternalOutput").ap()
    build(nc, t["x"], t["src"], t["dst"], t["edge_type_8"],
          [(t[f"W{n}l"], t[f"W{n}r"]) for n in (1, 2, 3)], [t[f"b{n}"] for n in (1, 2, 3)],
          [t["Wrel0"], t["Wrel1"]], [t["brel0"], t["brel1"]], out, n_edges, n_rel)
    r = run_bass_kernel_spmd(nc, [{f"in_{k}": a for k, a in arrays.items()}], core_ids=[0])
    return r.results[0]["out"][:n_nodes]
```

```python
from contextlib import ExitStack

import concourse.bass as bass
from concourse import mybir

P = 128
G = 7
LEAD = 3
COUNTS = (2, 4, G, G)
ALL, END = "all", "end"
SLOTS = 4
EPS = 1e-5


def build(nc, x, src, dst, edge_type, sage_w, sage_b, rel_w, rel_b, out, n_edges, n_rel):
    fp32, i32, u32 = mybir.dt.float32, mybir.dt.int32, mybir.dt.uint32
    ALU, ACT, AX = mybir.AluOpType, mybir.ActivationFunctionType, mybir.AxisListType

    n_pad, D = x.shape
    TILES = n_pad // P
    CHUNKS = src.shape[0] // P
    GROUPS = CHUNKS // G
    ROUNDS = GROUPS // SLOTS
    assert CHUNKS == ROUNDS * SLOTS * G and GROUPS <= P and CHUNKS <= 512
    DK = D // P
    CB = -(-CHUNKS // P)
    LAST = CHUNKS - (CB - 1) * P
    SAGE = len(sage_w)
    LAYERS = SAGE + len(rel_w)
    QR = 2
    QN = n_rel // QR
    RH = n_rel // 2
    DW = D + 1
    TB, KB, NB = 5, 2, 3
    assert TILES < 1 << TB and (GROUPS * (TILES - 1) << 2 * TB + NB) < 1 << 24
    ROW = GROUPS + 40
    EXTRA = 2
    X_BANK, TAIL_BANK = 3, 4

    ctx = ExitStack()
    with ctx:
        def sb(name, shape, dt):
            return ctx.enter_context(nc.sbuf_tensor(name, shape, dt))

        def sem(name):
            return ctx.enter_context(nc.semaphore(name))

        h_dram = [nc.dram_tensor(f"h{n}_rows", (n_pad, D), fp32).ap() for n in range(SAGE - 1)]
        x1_dram = nc.dram_tensor("x1_rows", (n_pad, D), fp32).ap()
        rel_dram = [nc.dram_tensor(f"rel{n}_rows", (n_rel, n_pad, D), fp32).ap() for n in range(LAYERS - SAGE)]
        sources = [x, *h_dram] + [r.rearrange("r n d -> (r n) d") for r in rel_dram]

        acc = sb("acc", [P, TILES, DW], fp32)
        right = sb("right", [P, TILES, D], fp32)
        src_cols = sb("src_cols", [P, CHUNKS], fp32)
        rel_cols = sb("rel_cols", [P, CHUNKS], fp32)
        dst_cols = sb("dst_cols", [P, CHUNKS], fp32)
        node_row = sb("node_row", [P, n_pad], fp32)
        ring = sb("ring", [P, SLOTS, G, DW], fp32)
        onehot = sb("onehot", [P, 3, G, P], fp32)
        idx = sb("idx", [P, SLOTS, G], u32)
        w_sage = sb("w_sage", [P, SAGE, 2, DK, D], fp32)
        w_rel = sb("w_rel", [P, DK, n_rel, D], fp32)
        bias_sage = sb("bias_sage", [P, SAGE, D], fp32)
        bias_rel = sb("bias_rel", [P, LAYERS - SAGE, D], fp32)
        ident = sb("ident", [P, P], fp32)
        reverse = sb("reverse", [P, P], fp32)
        ones = sb("ones", [1, P], fp32)
        zeros = sb("zeros", [P, DW], fp32)
        rdeg = sb("rdeg", [P, TILES], fp32)
        raw = sb("raw", [P, 3, CB, P], i32)
        raw_f = sb("raw_f", [P, 3, CB, P], fp32)
        by_group = sb("by_group", [GROUPS, G * P], i32)
        ends = sb("ends", [GROUPS, 3], fp32)
        by_chunk = sb("by_chunk", [GROUPS, 2, G], fp32)
        by_chunk_i = sb("by_chunk_i", [GROUPS, 2, G], i32)
        needs = sb("needs", [GROUPS, 3], fp32)
        plan = sb("plan", [1, 13, ROW], fp32)
        plan_i = sb("plan_i", [1, 3, GROUPS], i32)
        words = sb("words", [1, 2, GROUPS], i32)
        counts = sb("counts", [1, 1], i32)
        stats = sb("stats", [P, 6], fp32)
        mv = sb("mv", [P, 2], fp32)
        std = sb("std", [P, 2], fp32)
        x_tile = sb("x_tile", [P, D], fp32)
        xT = sb("xT", [P, D], fp32)
        entry = sb("entry", [P, D], fp32)
        meanT = sb("meanT", [P, D], fp32)
        h_new = sb("h_new", [P, D], fp32)
        x_res = sb("x_res", [P, D], fp32)
        turned = sb("turned", [P, D], fp32)
        rel_out = sb("rel_out", [P, 2, RH, D], fp32)

        ps = ctx.enter_context(nc.psum_tensor("ps", [P, 8, 512], fp32))
        ps_x = ps[:, X_BANK, 0:D]
        ps_tail = ps[:, TAIL_BANK, 0:D]
        rel_bank = [(*range(TAIL_BANK + 1, 8), X_BANK)[q % (8 - TAIL_BANK)] for q in range(QN)]
        ps_ends = ps[0:1, X_BANK, 0:3 * GROUPS].rearrange("p (e g) -> p e g", e=3)

        raw_loaded = [sem(f"raw_loaded{k}") for k in range(3)]
        ends_loaded = sem("ends_loaded")
        sage_w_loaded, bias_loaded = sem("sage_w_loaded"), sem("bias_loaded")
        rel_w_loaded = [sem(f"rel_w_loaded{n}") for n in range(LAYERS - SAGE)]
        identity_ready, constants = sem("identity_ready"), sem("constants")
        raw_floated, cols_turned = sem("raw_floated"), sem("cols_turned")
        src_ready, dst_ready, dst_masked, rel_cols_ready = (
            sem("src_ready"), sem("dst_ready"), sem("dst_masked"), sem("rel_cols_ready"))
        ends_found, ends_reversed = sem("ends_found"), sem("ends_reversed")
        dve_link, words_ready = sem("dve_link"), sem("words_ready")
        idx_ready = sem("idx_ready")
        landed = [[sem(f"landed{s}_{j}") for j in range(G)] for s in range(SLOTS)]
        first_marked, first_summed = sem("first_marked"), sem("first_summed")
        group_over = sem("group_over")
        cleared = sem("cleared")
        extra_marked = [sem(f"extra_marked{n}") for n in range(LAYERS)]
        extra_summed = [sem(f"extra_summed{n}") for n in range(LAYERS)]
        added = [sem(f"added{n}") for n in range(LAYERS)]
        waited = sem("waited")
        x_loaded, x_turned, x_kept = sem("x_loaded"), sem("x_turned"), sem("x_kept")
        deg_clamped, deg_ready = sem("deg_clamped"), sem("deg_ready")
        averaged, mean_turned, mean_kept = sem("averaged"), sem("mean_turned"), sem("mean_kept")
        y_ready, biased, h_ready = sem("y_ready"), sem("biased"), sem("h_ready")
        h_stored = sem("h_stored")
        tile_turned, tile_kept = sem("tile_turned"), sem("tile_kept")
        right_ready, right_kept = sem("right_ready"), sem("right_kept")
        copied = sem("copied")
        rel_ready = sem("rel_ready")
        rel_biased, rel_relu = sem("rel_biased"), sem("rel_relu")
        rel_stored = [sem(f"rel_stored_{h}") for h in range(2)]
        res_loaded, res_used = sem("res_loaded"), sem("res_used")
        stats_ready, aggregated = sem("stats_ready"), sem("aggregated")
        var_ready, std_ready, inverse_ready = sem("var_ready"), sem("std_ready"), sem("inverse_ready")
        out_stored = sem("out_stored")

        block = ctx.enter_context(nc.Block())

        def node_rows(dram, t):
            return dram[bass.ds(t * P, P), :]

        def tile_of(buffer, t, width):
            return buffer[:, bass.ds(t, 1), 0:width].rearrange("p a d -> p (a d)")

        def group_cols(cols, g):
            return cols[:, bass.ds(g * -G + (GROUPS - 1) * G, G)]

        def tile_number(k):
            return nc.s_assert_within(k, 0, TILES - 1,
                                      skip_runtime_bounds_check_because="the words hold numbers of tiles only")

        def wait_apart(eng):
            eng.sem_inc(waited, 1)

        def load_word(eng, n, g, bits):
            return eng.snap(eng.value_load(words[0:1, n, bass.ds(g, 1)], min_val=0, max_val=(1 << bits) - 1))

        def bits_of(word, low, width):
            return (word >> low) & ((1 << width) - 1)

        def layer_groups(eng, group, loads_unit, has_second):
            def whole_round(i):
                for s in range(SLOTS):
                    g = SLOTS * i + s
                    if isinstance(g, int) and g < 2:
                        group(g, s, i, 0, None, load_word(eng, 1, g, KB + 2 * TB + 1) if loads_unit else None)
                        continue
                    word = load_word(eng, 1, g, KB + 2 * TB + 1)
                    kind, k = bits_of(word, 0, KB), tile_number(bits_of(word, KB, TB))
                    with eng.If(kind == 1):
                        group(g, s, i, 1, k, word)
                    if has_second:
                        with eng.If(kind == 2):
                            group(g, s, i, 2, k, word)
                        with eng.If(kind == 0):
                            group(g, s, i, 0, None, word)
                    else:
                        with eng.If(kind != 1):
                            group(g, s, i, 0, None, word)
            whole_round(0)
            with eng.Fori(1, ROUNDS - 1) as i:
                whole_round(i)
            whole_round(ROUNDS - 1)

        def units_left(eng, taken, unit_of, has_second):
            with eng.Fori(taken, 2 * TILES) as unit:
                with eng.If((unit & 1) == 0):
                    unit_of(1, tile_number(unit >> 1))
                if has_second:
                    with eng.If((unit & 1) == 1):
                        unit_of(2, tile_number(unit >> 1))

        @block.sync
        def _(sp):
            full = (CB - 1) * P * P
            for k, e in enumerate((src, dst, edge_type)):
                sp.dma_start(raw[:, k, 0:CB - 1, :],
                             e[0:full].rearrange("(g p e) -> p g e", g=CB - 1, p=P)).then_inc(raw_loaded[k], 16)
                sp.dma_start(raw[0:LAST, k, CB - 1, :],
                             e[full:full + LAST * P].rearrange("(p e) -> p e", p=LAST)).then_inc(raw_loaded[k], 16)
                if k == 1:
                    sp.dma_start(by_group[:, :], e.rearrange("(g e) -> g e", g=GROUPS)).then_inc(ends_loaded, 16)
            for n, ws in enumerate(sage_w):
                for m, w in enumerate(ws):
                    sp.dma_start(w_sage[:, n, m, :, :],
                                 w.rearrange("(k p) o -> p k o", p=P)).then_inc(sage_w_loaded, 16)
            for n, b in enumerate(sage_b):
                sp.dma_start(bias_sage[:, n, :], b.partition_broadcast(P)).then_inc(bias_loaded, 16)
            for n, b in enumerate(rel_b):
                sp.dma_start(bias_rel[:, n, :], b.partition_broadcast(P)).then_inc(bias_loaded, 16)

            def load_rel_w(n):
                for k in range(DK):
                    sp.dma_start(w_rel[:, k, :, :],
                                 rel_w[n][:, k * P:(k + 1) * P, :].rearrange("r p o -> p r o")
                                 ).then_inc(rel_w_loaded[n], 16)
            load_rel_w(0)

            def store_h(dram, n, k, t):
                sp.wait_ge(h_ready, n * TILES + k + 1)
                sp.dma_start(node_rows(dram, t), h_new[:, :]).then_inc(
                    out_stored if dram is out else h_stored, 16)

            def store_rels(n, k, t):
                for h in range(2):
                    sp.wait_ge(rel_relu, (n * TILES + k) * 2 + h + 1)
                    sp.dma_start(rel_dram[n][RH * h:RH * (h + 1), bass.ds(t * P, P), :]
                                 .rearrange("r p d -> p r d"), rel_out[:, h, :, :]).then_inc(rel_stored[h], 16)

            sp.dma_start(x_tile[:, :], node_rows(x, TILES - 1)).then_inc(x_loaded, 16)
            with sp.Fori(0, TILES - 1) as k:
                t = sp.snap(k * -1 + (TILES - 1))
                sp.wait_ge(x_turned, k + 1)
                sp.dma_start(x_tile[:, :], node_rows(x, t - 1)).then_inc(x_loaded, 16)
                store_h(h_dram[0], 0, k, t)
            store_h(h_dram[0], 0, TILES - 1, 0)

            for n in range(1, SAGE - 1):
                with sp.Fori(0, TILES) as k:
                    store_h(h_dram[n], n, k, sp.snap(k * -1 + (TILES - 1)))

            n = SAGE - 1
            sp.dma_start(x_res[:, :], node_rows(x, TILES - 1)).then_inc(res_loaded, 16)
            with sp.Fori(0, TILES - 1) as k:
                t = sp.snap(k * -1 + (TILES - 1))
                sp.wait_ge(res_used, k + 1)
                sp.dma_start(x_res[:, :], node_rows(x, t - 1)).then_inc(res_loaded, 16)
                store_h(x1_dram, n, k, t)
                store_rels(0, k, t)
            store_h(x1_dram, n, TILES - 1, 0)
            store_rels(0, TILES - 1, 0)

            sp.wait_ge(rel_ready, QN * TILES)
            load_rel_w(1)
            with sp.Fori(0, TILES) as k:
                store_rels(1, k, sp.snap(k * -1 + (TILES - 1)))

            sp.wait_ge(h_stored, 16 * (SAGE * TILES + 1))
            sp.wait_ge(res_used, TILES)
            sp.dma_start(x_res[:, :], node_rows(x1_dram, TILES - 1)).then_inc(res_loaded, 16)
            with sp.Fori(0, TILES - 1) as k:
                t = sp.snap(k * -1 + (TILES - 1))
                sp.wait_ge(res_used, TILES + k + 1)
                sp.dma_start(x_res[:, :], node_rows(x1_dram, t - 1)).then_inc(res_loaded, 16)
                store_h(out, SAGE, k, t)
            store_h(out, SAGE, TILES - 1, 0)
            sp.wait_ge(out_stored, 16 * (TILES + 1))
            for h in range(2):
                sp.wait_ge(rel_stored[h], 16 * (2 * TILES + 1))

        @block.gpsimd
        def _(pool):
            pool.memset(zeros[:, :], 0.0).then_inc(constants, 1)
            pool.wait_ge(constants, 1)
            pool.affine_select(out=ident[:, :], in_=zeros[:, 0:P], compare_op=ALU.not_equal, fill=1.0,
                               base=0, pattern=[[-1, P]], channel_multiplier=1).then_inc(identity_ready, 1)
            pool.affine_select(out=reverse[:, :], in_=zeros[:, 0:P], compare_op=ALU.not_equal, fill=1.0,
                               base=1 - GROUPS, pattern=[[1, P]], channel_multiplier=1).then_inc(constants, 1)
            pool.memset(ones[:, :], 1.0).then_inc(constants, 1)
            pool.memset(ring[:, :, :, D:DW], 1.0).then_inc(constants, 1)
            pool.iota(node_row[:, :], pattern=[[1, n_pad]], base=0, channel_multiplier=0,
                      allow_small_or_imprecise_dtypes=True).then_inc(constants, 1)
            pool.wait_ge(dst_ready, 1)
            pool.affine_select(out=dst_cols[:, :], in_=dst_cols[:, :], compare_op=ALU.is_ge,
                               fill=-1.0, base=n_edges - 1, pattern=[[-P, CHUNKS]],
                               channel_multiplier=-1).then_inc(dst_masked, 1)

            for n in range(LAYERS):
                if 0 < n < SAGE:
                    pool.wait_ge(h_stored, 16 * (n * TILES + 1))
                elif n >= SAGE:
                    for h in range(2):
                        pool.wait_ge(rel_stored[h], 16 * ((n - SAGE + 1) * TILES + 1))
                with pool.Fori(0, ROUNDS) as i:
                    for s in range(SLOTS):
                        pool.wait_ge(idx_ready, n * GROUPS + SLOTS * i + s + 1)
                        wait_apart(pool)
                        for j in range(G):
                            pool.indirect_dma_start(
                                out=ring[:, s, j, 0:D], out_offset=None, in_=sources[n],
                                in_offset=bass.IndirectOffsetOnAxis(ap=idx[:, s, j:j + 1], axis=0),
                            ).then_inc(landed[s][j], 16)

        @block.scalar
        def _(act):
            def indices(n, g, s):
                cols = src_cols if n < SAGE else rel_cols
                act.activation(idx[:, s, :], group_cols(cols, g), ACT.Copy).then_inc(idx_ready, 1)

            def keep_turned(n, k):
                act.wait_ge(tile_turned, n * TILES + k + 1)
                if 0 < n < SAGE - 1 or n == SAGE - 1:
                    act.wait_ge(right_ready, min(n, SAGE - 1) * TILES if n == SAGE - 1 else n * TILES + k)
                act.activation(turned[:, :], ps_tail, ACT.Copy).then_inc(tile_kept, 1)

            def clear_tile(t):
                act.activation(tile_of(acc, t, DW), zeros[:, :], ACT.Copy).then_inc(cleared, 1)

            def tail(n, kind, k, over):
                t = None if k is None else k * -1 + (TILES - 1)
                if kind == 1 and n <= SAGE:
                    act.wait_ge(group_over, n * GROUPS + over)
                    if n < SAGE:
                        act.wait_ge(deg_ready, k + 1 if n == 0 else TILES)
                        act.activation(entry[:, :], tile_of(acc, t, D), ACT.Copy,
                                       scale=rdeg[:, bass.ds(t, 1)]).then_inc(averaged, 1)
                    else:
                        act.activation(entry[:, :], tile_of(acc, t, D), ACT.Copy).then_inc(copied, 1)
                if kind == 1 and n == 0:
                    act.wait_ge(x_turned, k + 1)
                    act.activation(xT[:, :], ps_x, ACT.Copy).then_inc(x_kept, 1)
                if kind == 1 and n < SAGE:
                    act.wait_ge(mean_turned, n * TILES + k + 1)
                    act.activation(meanT[:, :], ps_tail, ACT.Copy).then_inc(mean_kept, 1)
                    clear_tile(t)
                    if n < SAGE - 1:
                        act.wait_ge(biased, n * TILES + k + 1)
                        act.activation(h_new[:, :], h_new[:, :], ACT.Relu).then_inc(h_ready, 1)
                if kind == 1 and n in (SAGE - 1, LAYERS - 1):
                    act.wait_ge(var_ready, (n // SAGE) * TILES + k + 1)
                    act.activation(std[:, 0:1], std[:, 0:1], ACT.Sqrt).then_inc(std_ready, 1)
                if kind == 1 and n == SAGE - 1 or kind == 1 and n == SAGE or kind == 2 and n < SAGE - 1:
                    keep_turned(n, k)
                if kind == 1 and n == SAGE:
                    clear_tile(t)

            act.wait_ge(constants, 1)
            act.activation(acc[:, :, :], zeros[:, :].rearrange("p (a d) -> p a d", a=1).to_broadcast([P, TILES, DW]),
                           ACT.Copy).then_inc(cleared, 1)
            act.wait_ge(src_ready, 1)
            for n in range(LAYERS):
                if n > 0:
                    act.wait_ge(group_over, n * GROUPS)
                if n == SAGE:
                    act.wait_ge(rel_cols_ready, 1)
                for s in range(SLOTS):
                    indices(n, s, s)
                if n == 0:
                    act.wait_ge(words_ready, 1)

                def group(g, s, i, kind, k, word, n=n):
                    if not isinstance(g, int) or 1 <= g <= GROUPS - SLOTS:
                        act.wait_ge(group_over, n * GROUPS + g)
                        indices(n, g - 1 + SLOTS, (s - 1) % SLOTS)
                    tail(n, kind, k, g)
                layer_groups(act, group, False, n < LAYERS - 1)
                taken = act.value_load(counts[0:1, 0:1], min_val=0, max_val=2 * TILES - 2)
                units_left(act, taken, lambda kind, k, n=n: tail(n, kind, k, GROUPS), n < LAYERS - 1)

        @block.tensor
        def _(pe):
            def turn(target, source):
                for d in range(DK):
                    last = pe.transpose(target[:, d * P:(d + 1) * P], source[:, d * P:(d + 1) * P], ident[:, :])
                return last

            def multiply(target, source, w, start=True, stop=True):
                for d in range(DK):
                    last = pe.matmul(target, source[:, d * P:(d + 1) * P], w[d],
                                     start=start and d == 0, stop=stop and d == DK - 1)
                return last

            def sage_weights(n, m):
                return [w_sage[:, n, m, d, :] for d in range(DK)]

            def rel_product(m, k, q):
                before = max(p for p in range(-QN, q) if rel_bank[p % QN] == rel_bank[q])
                pe.wait_ge(rel_biased, (m * TILES + k + 1) * QN + before + 1)
                multiply(ps[:, rel_bank[q], :], turned,
                         [w_rel[:, d, q * QR:(q + 1) * QR, :].rearrange("p r o -> p (r o)")
                          for d in range(DK)]).then_inc(rel_ready, 1)

            def turn_new(n, k):
                pe.wait_ge(h_ready, n * TILES + k + 1)
                turn(ps_tail, h_new).then_inc(tile_turned, 1)

            def tail(n, kind, k, j):
                if kind == 1 and n < SAGE:
                    if j == 2:
                        if n == 0:
                            pe.wait_ge(x_loaded, 16 * (k + 1))
                            turn(ps_x, x_tile).then_inc(x_turned, 1)
                        pe.wait_ge(right_kept, n * TILES + k + 1 if n < SAGE - 1 else n * TILES + 1)
                        pe.wait_ge(averaged, n * TILES + k + 1)
                        turn(ps_tail, entry).then_inc(mean_turned, 1)
                    if j == END:
                        pe.wait_ge(mean_kept, n * TILES + k + 1)
                        multiply(ps_tail, meanT, sage_weights(n, 0), stop=n > 0).then_inc(y_ready if n else waited, 1)
                        if n == 0:
                            pe.wait_ge(x_kept, k + 1)
                            multiply(ps_tail, xT, sage_weights(0, 1), start=False).then_inc(y_ready, 1)
                if kind == 2 and n < SAGE - 1:
                    if j == 2:
                        turn_new(n, k)
                    if j == END:
                        pe.wait_ge(tile_kept, n * TILES + k + 1)
                        multiply(ps_tail, turned, sage_weights(n + 1, 1)).then_inc(right_ready, 1)
                if kind == 2 and n == SAGE - 1:
                    if j == ALL:
                        turn_new(n, k)
                    if j == END:
                        pe.wait_ge(tile_kept, n * TILES + k + 1)
                        for q in range(QN):
                            rel_product(0, k, q)
                if n == SAGE:
                    if kind == 1 and j == 2:
                        pe.wait_ge(copied, k + 1)
                        turn(ps_tail, entry).then_inc(tile_turned, 1)
                    if kind == 1 and j == END:
                        pe.wait_ge(tile_kept, n * TILES + k + 1)
                        rel_product(1, k, 0)
                        rel_product(1, k, 1)
                    if kind == 2 and j in (0, END):
                        rel_product(1, k, 3 if j == END else 2)

            pe.wait_ge(identity_ready, 1)
            for k in range(3):
                pe.wait_ge(raw_floated, k + 1)
                for b in range(CB):
                    n = LAST if b == CB - 1 else P
                    last = pe.transpose(ps[:, k, b * P:b * P + n], raw_f[0:n, k, b, :], ident[0:n, 0:n])
                last.then_inc(cols_turned, 1)
                if k == 1:
                    pe.wait_ge(constants, 5)
                    pe.wait_ge(ends_found, 1)
                    for e in range(3):
                        last = pe.matmul(ps_ends[:, e, :], ends[:, e:e + 1], reverse[0:GROUPS, 0:GROUPS],
                                         start=True, stop=True)
                    last.then_inc(ends_reversed, 1)
            pe.wait_ge(words_ready, 1)
            pe.wait_ge(rel_cols_ready, 1)

            for n in range(LAYERS):
                if n in (SAGE - 1, SAGE):
                    pe.wait_ge(rel_w_loaded[n - SAGE + 1], 16 * DK)
                if n == 0:
                    pe.wait_ge(sage_w_loaded, 16 * 2 * SAGE)

                def group(g, s, i, kind, k, word, n=n):
                    h = s % 2
                    span_word = load_word(pe, 0, g, 24)
                    before, extra = span_word >> (2 * TB + NB), bits_of(span_word, NB, TB)
                    needed = bits_of(span_word, 0, NB)
                    pe.wait_ge(first_marked, n * GROUPS + g + 1)
                    if n > 0 or not isinstance(g, int) or g >= 2:
                        pe.wait_ge(group_over, n * GROUPS + g - 1)

                    def product(j, start=False, stop=False):
                        pe.wait_ge(landed[s][j], 16 * (n * ROUNDS + i + 1))
                        return pe.matmul(ps[:, h, 0:DW], onehot[:, h, j, :], ring[:, s, j, :],
                                         start=start, stop=stop)
                    for j in range(LEAD, G - 1):
                        product(j, start=j == LEAD)
                        tail(n, kind, k, j - LEAD)
                    with pe.If(needed > 3):
                        product(G - 1)
                        for j in range(LEAD):
                            last = product(j, stop=j == LEAD - 1)
                        last.then_inc(first_summed, 1)
                    with pe.If(needed < 4):
                        for j in range(LEAD):
                            pe.wait_ge(landed[s][j], 16 * (n * ROUNDS + i + 1))
                        product(G - 1, stop=True).then_inc(first_summed, 1)
                    tail(n, kind, k, ALL)
                    with pe.If(extra > 0):
                        with pe.Fori(before + 1, before + extra + 1) as number:
                            pe.wait_ge(extra_marked[n], number)

                            def products(count):
                                for j in range(count):
                                    last = pe.matmul(ps[:, EXTRA, 0:DW], onehot[:, EXTRA, j, :], ring[:, s, j, :],
                                                     start=(j == 0), stop=(j == count - 1))
                                last.then_inc(extra_summed[n], 1)
                            for code, count in enumerate(COUNTS):
                                with pe.If((needed & 3) == code):
                                    products(count)
                    tail(n, kind, k, END)
                layer_groups(pe, group, False, n < LAYERS - 1)
                if n < LAYERS - 1:
                    taken = pe.value_load(counts[0:1, 0:1], min_val=0, max_val=2 * TILES - 2)

                    def unit(kind, k, n=n):
                        for j in (*range(G), ALL, END):
                            tail(n, kind, k, j)
                    units_left(pe, taken, unit, True)

        @block.vector
        def _(dve):
            linked = [0]

            def link(ins):
                linked[0] += 1
                ins.then_inc(dve_link, 1)
                dve.wait_ge(dve_link, linked[0])

            dve.sem_inc(rel_biased, QN)
            dve.sem_inc(right_kept, 1)
            for ahead in (h_stored, *rel_stored, out_stored):
                dve.sem_inc(ahead, 16)

            for k in range(3):
                dve.wait_ge(raw_loaded[k], 32)
                dve.tensor_copy(raw_f[:, k, 0:CB - 1, :], raw[:, k, 0:CB - 1, :])
                dve.tensor_copy(raw_f[0:LAST, k, CB - 1, :], raw[0:LAST, k, CB - 1, :]).then_inc(raw_floated, 1)
                if k == 1:
                    dve.wait_ge(cols_turned, 1)
                    dve.tensor_copy(src_cols[:, :], ps[:, 0, 0:CHUNKS]).then_inc(src_ready, 1)
            dve.wait_ge(cols_turned, 2)
            dve.tensor_copy(dst_cols[:, :], ps[:, 1, 0:CHUNKS]).then_inc(dst_ready, 1)
            dve.wait_ge(ends_loaded, 16)
            chunked = by_group[:, :].rearrange("g (c p) -> g c p", c=G)
            link(dve.tensor_reduce(by_chunk[:, 0, :], chunked, axis=AX.X, op=ALU.max))
            link(dve.tensor_reduce(by_chunk[:, 1, :], chunked, axis=AX.X, op=ALU.min))
            link(dve.tensor_copy(by_chunk_i[:, :, :], by_chunk[:, :, :]))
            link(dve.tensor_scalar(by_chunk_i[:, :, :], by_chunk_i[:, :, :], P.bit_length() - 1, None,
                                   op0=ALU.arith_shift_right))
            link(dve.tensor_copy(by_chunk[:, :, :], by_chunk_i[:, :, :]))
            link(dve.tensor_reduce(ends[:, 0:1], by_chunk[:, 0, :], axis=AX.X, op=ALU.max))
            link(dve.tensor_reduce(ends[:, 1:2], by_chunk[:, 1, :], axis=AX.X, op=ALU.min))
            link(dve.tensor_reduce(needs[:, 0:1], by_chunk[:, 0, 0:LEAD], axis=AX.X, op=ALU.max))
            link(dve.tensor_reduce(needs[:, 1:2], by_chunk[:, 1, COUNTS[1]:G], axis=AX.X, op=ALU.min))
            link(dve.tensor_reduce(needs[:, 2:3], by_chunk[:, 1, COUNTS[0]:G], axis=AX.X, op=ALU.min))
            link(dve.tensor_tensor(needs[:, 0:1], needs[:, 0:1], ends[:, 0:1], op=ALU.is_ge))
            link(dve.tensor_tensor(needs[:, 1:3], needs[:, 1:3], ends[:, 0:1].to_broadcast([GROUPS, 2]),
                                   op=ALU.is_lt))
            link(dve.scalar_tensor_tensor(needs[:, 0:1], needs[:, 0:1], 2.0, needs[:, 1:2],
                                          op0=ALU.mult, op1=ALU.add))
            dve.scalar_tensor_tensor(ends[:, 2:3], needs[:, 0:1], 2.0, needs[:, 2:3],
                                     op0=ALU.mult, op1=ALU.add).then_inc(ends_found, 1)

            (high, extra, through, before, word, avail, taken_by, change, shifted, other, unit_row, low, needed) = (
                plan[0:1, n, :] for n in range(13))
            link(dve.memset(plan[:, :, :], 0.0))
            dve.wait_ge(ends_reversed, 1)
            link(dve.tensor_copy(high[:, 0:GROUPS], ps_ends[:, 0, :]))
            link(dve.tensor_copy(low[:, 0:GROUPS], ps_ends[:, 1, :]))
            link(dve.tensor_copy(needed[:, 0:GROUPS], ps_ends[:, 2, :]))
            dve.wait_ge(constants, 5)
            link(dve.tensor_tensor(extra[:, 0:GROUPS], high[:, 0:GROUPS], low[:, 0:GROUPS], op=ALU.subtract))
            link(dve.tensor_tensor_scan(through[:, 0:GROUPS], extra[:, 0:GROUPS], zeros[0:1, 0:GROUPS], 0.0,
                                        op0=ALU.add, op1=ALU.add))
            link(dve.tensor_tensor(before[:, 0:GROUPS], through[:, 0:GROUPS], extra[:, 0:GROUPS], op=ALU.subtract))
            link(dve.scalar_tensor_tensor(word[:, 0:GROUPS], before[:, 0:GROUPS], float(1 << TB), high[:, 0:GROUPS],
                                          op0=ALU.mult, op1=ALU.add))
            link(dve.scalar_tensor_tensor(word[:, 0:GROUPS], word[:, 0:GROUPS], float(1 << TB), extra[:, 0:GROUPS],
                                          op0=ALU.mult, op1=ALU.add))
            link(dve.scalar_tensor_tensor(words[0:1, 0, :], word[:, 0:GROUPS], float(1 << NB), needed[:, 0:GROUPS],
                                          op0=ALU.mult, op1=ALU.add))
            link(dve.tensor_copy(shifted[:, 0:GROUPS], high[:, 0:GROUPS]))
            rows, step = [shifted, other], 1
            while step < GROUPS:
                link(dve.tensor_tensor(rows[1][:, 0:GROUPS], rows[0][:, 0:GROUPS], rows[0][:, step:step + GROUPS],
                                       op=ALU.max))
                rows, step = rows[::-1], 2 * step
            link(dve.tensor_scalar(avail[:, 2:GROUPS], rows[0][:, 2:GROUPS], -2.0, 2.0 * (TILES - 1),
                                   op0=ALU.mult, op1=ALU.add))
            link(dve.tensor_tensor_scan(taken_by[:, 1:GROUPS + 1], ones[0:1, 0:GROUPS], avail[:, 0:GROUPS], 0.0,
                                        op0=ALU.add, op1=ALU.min))
            link(dve.tensor_copy(counts[0:1, 0:1], taken_by[:, GROUPS:GROUPS + 1]))
            link(dve.tensor_tensor(change[:, 0:GROUPS], taken_by[:, 1:GROUPS + 1], taken_by[:, 0:GROUPS],
                                   op=ALU.subtract))
            unit_i, tile_i, second_i = (plan_i[0:1, n, :] for n in range(3))
            link(dve.tensor_copy(unit_i, taken_by[:, 0:GROUPS]))
            link(dve.tensor_scalar(tile_i, unit_i, 1, None, op0=ALU.arith_shift_right))
            link(dve.tensor_scalar(second_i, unit_i, 1, None, op0=ALU.bitwise_and))
            link(dve.scalar_tensor_tensor(unit_row[:, 0:GROUPS], tile_i, float(1 << KB), second_i,
                                          op0=ALU.mult, op1=ALU.add))
            link(dve.scalar_tensor_tensor(unit_row[:, 0:GROUPS], unit_row[:, 0:GROUPS], 1.0, change[:, 0:GROUPS],
                                          op0=ALU.add, op1=ALU.mult))
            link(dve.scalar_tensor_tensor(unit_row[:, 0:GROUPS], high[:, 1:GROUPS + 1], float(1 << KB + TB),
                                          unit_row[:, 0:GROUPS], op0=ALU.mult, op1=ALU.add))
            link(dve.tensor_scalar(extra[:, 0:GROUPS], extra[:, 0:GROUPS], 1.0, float(1 << KB + 2 * TB),
                                   op0=ALU.min, op1=ALU.mult))
            link(dve.tensor_tensor(words[0:1, 1, :], extra[:, 1:GROUPS + 1], unit_row[:, 0:GROUPS], op=ALU.add))
            dve.sem_inc(words_ready, 1)

            dve.wait_ge(cols_turned, 3)
            dve.scalar_tensor_tensor(rel_cols[:, :], ps[:, 2, 0:CHUNKS], float(n_pad), src_cols[:, :],
                                     op0=ALU.mult, op1=ALU.add).then_inc(rel_cols_ready, 1)
            dve.wait_ge(dst_masked, 1)
            dve.wait_ge(bias_loaded, 16 * LAYERS)

            def mark(buffer, g, t):
                return dve.tensor_tensor(
                    onehot[:, buffer, :, :],
                    node_row[:, bass.ds(t * P, P)].rearrange("p (a d) -> p a d", a=1).to_broadcast([P, G, P]),
                    group_cols(dst_cols, g).rearrange("p (g a) -> p g a", a=1).to_broadcast([P, G, P]),
                    op=ALU.is_equal)

            def mark_extra(n, g, t):
                mark(EXTRA, g, tile_number(t)).then_inc(extra_marked[n], 1)

            def add(n, bank, t):
                dve.tensor_tensor(tile_of(acc, t, DW), tile_of(acc, t, DW), ps[:, bank, 0:DW],
                                  op=ALU.add).then_inc(added[n], 1)

            def bias_rel_product(m, k, q):
                dve.wait_ge(rel_ready, (m * TILES + k) * QN + q + 1)
                if q % (QN // 2) == 0:
                    dve.wait_ge(rel_stored[2 * q // QN], 16 * (m * TILES + k + 1))
                part = rel_out[:, q * QR // RH, q * QR % RH:q * QR % RH + QR, :]
                dve.tensor_tensor(part, ps[:, rel_bank[q], :].rearrange("p (r d) -> p r d", r=QR),
                                  bias_rel[:, m:m + 1, :].to_broadcast([P, QR, D]),
                                  op=ALU.add).then_inc(rel_biased, 1)
                if q % (QN // 2) == QN // 2 - 1:
                    half = rel_out[:, 2 * q // QN, :, :]
                    dve.wait_ge(rel_biased, (m * TILES + k + 1) * QN + q + 1)
                    dve.tensor_scalar(half, half, 0.0, None, op0=ALU.max).then_inc(rel_relu, 1)

            def layer_norm(m, k):
                done = m * TILES + k + 1
                dve.wait_ge(res_used, done)
                dve.bn_stats(stats[:, :], h_new[:, :]).then_inc(stats_ready, 1)
                dve.wait_ge(stats_ready, done)
                wait_apart(dve)
                dve.bn_aggr(mv[:, :], stats[:, :]).then_inc(aggregated, 1)
                dve.wait_ge(aggregated, done)
                dve.tensor_scalar(std[:, 0:1], mv[:, 1:2], EPS, None, op0=ALU.add).then_inc(var_ready, 1)
                dve.wait_ge(std_ready, done)
                dve.reciprocal(std[:, 1:2], std[:, 0:1]).then_inc(inverse_ready, 1)
                dve.wait_ge(inverse_ready, done)
                dve.tensor_scalar(h_new[:, :], h_new[:, :], mv[:, 0:1], std[:, 1:2],
                                  op0=ALU.subtract, op1=ALU.mult).then_inc(h_ready, 1)

            def degrees(k, over):
                t = k * -1 + (TILES - 1)
                factor = rdeg[:, bass.ds(t, 1)]
                dve.wait_ge(group_over, over)
                dve.tensor_scalar(factor, acc[:, bass.ds(t, 1), D:DW].rearrange("p a d -> p (a d)"), 1.0, None,
                                  op0=ALU.max).then_inc(deg_clamped, 1)
                dve.wait_ge(deg_clamped, k + 1)
                wait_apart(dve)
                dve.reciprocal(factor, factor).then_inc(deg_ready, 1)

            def tail(n, kind, k, over):
                t = None if k is None else k * -1 + (TILES - 1)
                if kind == 1 and n < SAGE:
                    dve.wait_ge(y_ready, n * TILES + k + 1)
                    dve.wait_ge(h_stored, 16 * (n * TILES + k + 1))
                    dve.tensor_tensor(h_new[:, :], ps_tail, bias_sage[:, 0, :] if n == 0 else tile_of(right, t, D),
                                      op=ALU.add).then_inc(biased, 1)
                    if n == SAGE - 1:
                        dve.wait_ge(biased, n * TILES + k + 1)
                        dve.wait_ge(res_loaded, 16 * (k + 1))
                        dve.tensor_tensor(h_new[:, :], h_new[:, :], x_res[:, :], op=ALU.add).then_inc(res_used, 1)
                        layer_norm(0, k)
                if kind == 2 and n < SAGE - 1:
                    dve.wait_ge(right_ready, n * TILES + k + 1)
                    dve.tensor_tensor(tile_of(right, t, D), ps_tail, bias_sage[:, n + 1, :],
                                      op=ALU.add).then_inc(right_kept, 1)
                if kind == 2 and n == SAGE - 1:
                    for q in range(QN):
                        bias_rel_product(0, k, q)
                if n == SAGE:
                    for q in ([], [0], range(1, QN))[kind]:
                        bias_rel_product(1, k, q)
                if n == LAYERS - 1 and kind == 1:
                    dve.wait_ge(group_over, n * GROUPS + over)
                    dve.wait_ge(res_loaded, 16 * (TILES + k + 1))
                    dve.wait_ge(out_stored, 16 * (k + 1))
                    dve.tensor_tensor(h_new[:, :], tile_of(acc, t, D), x_res[:, :], op=ALU.add).then_inc(res_used, 1)
                    layer_norm(1, k)

            for n in range(LAYERS):
                span_word = load_word(dve, 0, 0, 24)
                high = bits_of(span_word, NB + TB, TB)
                mark(0, 0, tile_number(high)).then_inc(first_marked, 1)
                with dve.If(bits_of(span_word, NB, TB) > 0):
                    mark_extra(n, 0, high - 1)
                dve.wait_ge(cleared, n * TILES + 1)
                if n == LAYERS - 1:
                    dve.wait_ge(h_stored, 16 * (SAGE * TILES + 1))

                def group(g, s, i, kind, k, word, n=n):
                    h = s % 2
                    span_word = load_word(dve, 0, g, 24)
                    before, extra = span_word >> (2 * TB + NB), bits_of(span_word, NB, TB)
                    high = tile_number(bits_of(span_word, NB + TB, TB))
                    if not (isinstance(g, int) and g == GROUPS - 1):
                        mark(1 - h, g + 1, tile_number(bits_of(word, KB + TB, TB))).then_inc(first_marked, 1)
                    if kind == 1 and n == 0:
                        degrees(k, g)
                    dve.wait_ge(first_summed, n * GROUPS + g + 1)
                    if not (isinstance(g, int) and g == 0):
                        dve.wait_ge(added[n], before + g)
                    add(n, h, high)
                    with dve.If(extra > 0):
                        dve.wait_ge(extra_summed[n], before + 1)
                        dve.wait_ge(added[n], before + g + 1)
                        add(n, EXTRA, tile_number(high - 1))
                        with dve.If(extra > 1):
                            with dve.Fori(before + 2, before + extra + 1) as number:
                                t = high + before - number
                                mark_extra(n, g, t)
                                dve.wait_ge(extra_summed[n], number)
                                dve.wait_ge(added[n], number + g)
                                add(n, EXTRA, tile_number(t))
                    dve.wait_ge(added[n], before + extra + g + 1)
                    dve.sem_inc(group_over, 1)
                    if not (isinstance(g, int) and g == GROUPS - 1):
                        with dve.If((word >> (KB + 2 * TB)) > 0):
                            mark_extra(n, g + 1, bits_of(word, KB + TB, TB) - 1)
                    tail(n, kind, k, g)
                layer_groups(dve, group, True, n < LAYERS - 1)
                taken = dve.value_load(counts[0:1, 0:1], min_val=0, max_val=2 * TILES - 2)
                
                def unit(kind, k, n=n):
                    if kind == 1 and n == 0:
                        degrees(k, GROUPS)
                    tail(n, kind, k, GROUPS)
                units_left(dve, taken, unit, n < LAYERS - 1)


def kernel(**inputs):
    import numpy as np
    import concourse.bacc as bacc
    from concourse.bass_utils import run_bass_kernel_spmd

    x = np.asarray(inputs["x"])
    n_nodes, d = x.shape
    n_edges = inputs["src"].shape[0]
    w_rel = [np.ascontiguousarray(inputs[f"L1_gnn_W{n}"]) for n in range(2)]
    n_rel = w_rel[0].shape[0]
    arrays = {
        "x": np.pad(x, ((0, -n_nodes % P), (0, 0))),
        **{k: np.pad(np.asarray(inputs[k]), (0, -n_edges % (SLOTS * G * P)), mode="edge") for k in ("src", "dst", "edge_type_8")},
        **{f"W{n}{s}": np.ascontiguousarray(np.asarray(inputs[f"L0_gnn_W{n}{s}"]).T) for n in (1, 2, 3) for s in "lr"},
        **{f"b{n}": np.asarray(inputs[f"L0_gnn_b{n}l"]) for n in (1, 2, 3)},
        **{f"Wrel{n}": w_rel[n] for n in range(2)},
        **{f"brel{n}": np.asarray(inputs[f"L1_gnn_b{n}"]) for n in range(2)},
    }
    nc = bacc.Bacc("TRN2", target_bir_lowering=False, num_devices=1)
    t = {k: nc.dram_tensor(f"in_{k}", a.shape, mybir.dt.from_np(a.dtype), kind="ExternalInput").ap()
         for k, a in arrays.items()}
    out = nc.dram_tensor("out", arrays["x"].shape, mybir.dt.float32, kind="ExternalOutput").ap()
    build(nc, t["x"], t["src"], t["dst"], t["edge_type_8"],
          [(t[f"W{n}l"], t[f"W{n}r"]) for n in (1, 2, 3)], [t[f"b{n}"] for n in (1, 2, 3)],
          [t["Wrel0"], t["Wrel1"]], [t["brel0"], t["brel1"]], out, n_edges, n_rel)
    r = run_bass_kernel_spmd(nc, [{f"in_{k}": a for k, a in arrays.items()}], core_ids=[0])
    return r.results[0]["out"][:n_nodes]
```

```python
from contextlib import ExitStack

import concourse.bass as bass
from concourse import mybir

P = 128
G = 7
LEAD = 3
COUNTS = (2, 4, G, G)
ALL, END = "all", "end"
SLOTS = 4
EPS = 1e-5


def build(nc, x, src, dst, edge_type, sage_w, sage_b, rel_w, rel_b, out, n_rel):
    fp32, i32, u32 = mybir.dt.float32, mybir.dt.int32, mybir.dt.uint32
    ALU, ACT, AX = mybir.AluOpType, mybir.ActivationFunctionType, mybir.AxisListType

    n_pad, D = x.shape
    TILES = n_pad // P
    CHUNKS = src.shape[0] // P
    GROUPS = CHUNKS // G
    ROUNDS = GROUPS // SLOTS
    assert CHUNKS == ROUNDS * SLOTS * G and GROUPS <= P and CHUNKS <= 512
    DK = D // P
    CB = -(-CHUNKS // P)
    LAST = CHUNKS - (CB - 1) * P
    SAGE = len(sage_w)
    LAYERS = SAGE + len(rel_w)
    QR = 2
    QN = n_rel // QR
    RH = n_rel // 2
    DW = D + 1
    TB, KB, NB = 5, 2, 3
    WORD_BITS = KB + 4 * TB + 1
    assert WORD_BITS < 24 and TILES < 1 << TB and (GROUPS * (TILES - 1) << 2 * TB + NB) < 1 << 24
    ROW = GROUPS + 40
    EXTRA = 2
    X_BANK, TAIL_BANK = 3, 4

    ctx = ExitStack()
    with ctx:
        def sb(name, shape, dt):
            return ctx.enter_context(nc.sbuf_tensor(name, shape, dt))

        def sem(name):
            return ctx.enter_context(nc.semaphore(name))

        h_dram = [nc.dram_tensor(f"h{n}_rows", (n_pad, D), fp32).ap() for n in range(SAGE - 1)]
        x1_dram = nc.dram_tensor("x1_rows", (n_pad, D), fp32).ap()
        rel_dram = [nc.dram_tensor(f"rel{n}_rows", (n_rel, n_pad, D), fp32).ap() for n in range(LAYERS - SAGE)]
        sources = [x, *h_dram] + [r.rearrange("r n d -> (r n) d") for r in rel_dram]

        acc = sb("acc", [P, TILES, DW], fp32)
        right = sb("right", [P, TILES, D], fp32)
        src_cols = sb("src_cols", [P, CHUNKS], fp32)
        rel_cols = sb("rel_cols", [P, CHUNKS], fp32)
        dst_cols = sb("dst_cols", [P, CHUNKS], fp32)
        node_row = sb("node_row", [P, n_pad], fp32)
        ring = sb("ring", [P, SLOTS, G, DW], fp32)
        onehot = sb("onehot", [P, 3, G, P], fp32)
        idx = sb("idx", [P, SLOTS, G], u32)
        w_sage = sb("w_sage", [P, SAGE, 2, DK, D], fp32)
        w_rel = sb("w_rel", [P, LAYERS - SAGE, DK, n_rel, D], fp32)
        bias_sage = sb("bias_sage", [P, SAGE, D], fp32)
        bias_rel = sb("bias_rel", [P, LAYERS - SAGE, D], fp32)
        ident = sb("ident", [P, P], fp32)
        reverse = sb("reverse", [P, P], fp32)
        ones = sb("ones", [1, P], fp32)
        zeros = sb("zeros", [P, DW], fp32)
        eps = sb("eps", [P, 1], fp32)
        first_root = sb("first_root", [P, 1], fp32)
        rdeg = sb("rdeg", [P, TILES], fp32)
        raw = sb("raw", [P, 3, CB, P], i32)
        raw_f = sb("raw_f", [P, 3, CB, P], fp32)
        by_group = sb("by_group", [GROUPS, G * P], i32)
        ends = sb("ends", [GROUPS, 3], fp32)
        by_chunk = sb("by_chunk", [GROUPS, 2, G], fp32)
        by_chunk_i = sb("by_chunk_i", [GROUPS, 2, G], i32)
        needs = sb("needs", [GROUPS, 3], fp32)
        plan = sb("plan", [1, 13, ROW], fp32)
        plan_i = sb("plan_i", [1, 3, GROUPS], i32)
        words = sb("words", [1, 2, GROUPS], i32)
        counts = sb("counts", [1, 1], i32)
        stats = sb("stats", [P, 6], fp32)
        mv = sb("mv", [P, 2], fp32)
        std = sb("std", [P, 2], fp32)
        x_tile = sb("x_tile", [P, D], fp32)
        xT = sb("xT", [P, D], fp32)
        entry = sb("entry", [P, D], fp32)
        sumsT = sb("sumsT", [P, D], fp32)
        h_new = sb("h_new", [P, D], fp32)
        z_new = sb("z_new", [P, D], fp32)
        x_res = sb("x_res", [P, D], fp32)
        turned = sb("turned", [P, D], fp32)
        rel_out = sb("rel_out", [P, 2, RH, D], fp32)

        ps = ctx.enter_context(nc.psum_tensor("ps", [P, 8, 512], fp32))
        ps_x = ps[:, X_BANK, 0:D]
        ps_tail = ps[:, TAIL_BANK, 0:D]
        rel_bank = [(*range(TAIL_BANK + 1, 8), X_BANK)[q % (8 - TAIL_BANK)] for q in range(QN)]
        ps_ends = ps[0:1, X_BANK, 0:3 * GROUPS].rearrange("p (e g) -> p e g", e=3)

        raw_loaded = [sem(f"raw_loaded{k}") for k in range(3)]
        ends_loaded = sem("ends_loaded")
        sage_w_loaded, bias_loaded = sem("sage_w_loaded"), sem("bias_loaded")
        rel_w_loaded = [sem(f"rel_w_loaded{n}") for n in range(LAYERS - SAGE)]
        identity_ready, constants = sem("identity_ready"), sem("constants")
        raw_floated, cols_turned = sem("raw_floated"), sem("cols_turned")
        src_ready, dst_ready, rel_cols_ready = sem("src_ready"), sem("dst_ready"), sem("rel_cols_ready")
        ends_found, ends_reversed = sem("ends_found"), sem("ends_reversed")
        dve_link, words_ready = sem("dve_link"), sem("words_ready")
        idx_ready = sem("idx_ready")
        landed = [[sem(f"landed{s}_{j}") for j in range(G)] for s in range(SLOTS)]
        first_marked, first_summed = sem("first_marked"), sem("first_summed")
        group_over = sem("group_over")
        cleared = sem("cleared")
        extra_marked = [sem(f"extra_marked{n}") for n in range(LAYERS)]
        extra_summed = [sem(f"extra_summed{n}") for n in range(LAYERS)]
        added = [sem(f"added{n}") for n in range(LAYERS)]
        waited = sem("waited")
        x_loaded, x_turned, x_kept = sem("x_loaded"), sem("x_turned"), sem("x_kept")
        deg_clamped, deg_ready = sem("deg_clamped"), sem("deg_ready")
        sums_turned, sums_kept, x_right_ready = sem("sums_turned"), sem("sums_kept"), sem("x_right_ready")
        z_ready, z_kept = sem("z_ready"), sem("z_kept")
        y_ready, biased, h_ready = sem("y_ready"), sem("biased"), sem("h_ready")
        h_stored = sem("h_stored")
        tile_turned, tile_kept = sem("tile_turned"), sem("tile_kept")
        right_ready, right_kept = sem("right_ready"), sem("right_kept")
        copied = sem("copied")
        rel_ready = sem("rel_ready")
        rel_biased, rel_relu = sem("rel_biased"), sem("rel_relu")
        rel_stored = [sem(f"rel_stored_{h}") for h in range(2)]
        res_loaded, res_biased, res_used = sem("res_loaded"), sem("res_biased"), sem("res_used")
        stats_ready, aggregated = sem("stats_ready"), sem("aggregated")
        std_ready, inverse_ready = sem("std_ready"), sem("inverse_ready")
        out_stored = sem("out_stored")

        block = ctx.enter_context(nc.Block())

        def node_rows(dram, t):
            return dram[bass.ds(t * P, P), :]

        def tile_of(buffer, t, width):
            return buffer[:, bass.ds(t, 1), 0:width].rearrange("p a d -> p (a d)")

        def group_cols(cols, g):
            return cols[:, bass.ds(g * -G + (GROUPS - 1) * G, G)]

        def tile_number(k):
            return nc.s_assert_within(k, 0, TILES - 1,
                                      skip_runtime_bounds_check_because="the words hold numbers of tiles only")

        def wait_apart(eng):
            eng.sem_inc(waited, 1)

        def load_word(eng, n, g, bits):
            return eng.snap(eng.value_load(words[0:1, n, bass.ds(g, 1)], min_val=0, max_val=(1 << bits) - 1))

        def bits_of(word, low, width):
            return (word >> low) & ((1 << width) - 1)

        def layer_groups(eng, group, loads_unit, has_second):
            def whole_round(i):
                for s in range(SLOTS):
                    g = SLOTS * i + s
                    if isinstance(g, int) and g < 2:
                        group(g, s, i, 0, None, load_word(eng, 1, g, WORD_BITS) if loads_unit else None)
                        continue
                    word = load_word(eng, 1, g, WORD_BITS)
                    kind, k = bits_of(word, 0, KB), tile_number(bits_of(word, KB, TB))
                    with eng.If(kind == 1):
                        group(g, s, i, 1, k, word)
                    if has_second:
                        with eng.If(kind == 2):
                            group(g, s, i, 2, k, word)
                        with eng.If(kind == 0):
                            group(g, s, i, 0, None, word)
                    else:
                        with eng.If(kind != 1):
                            group(g, s, i, 0, None, word)
            whole_round(0)
            with eng.Fori(1, ROUNDS - 1) as i:
                whole_round(i)
            whole_round(ROUNDS - 1)

        def units_left(eng, taken, unit_of, has_second):
            with eng.Fori(taken, 2 * TILES) as unit:
                with eng.If((unit & 1) == 0):
                    unit_of(1, tile_number(unit >> 1))
                if has_second:
                    with eng.If((unit & 1) == 1):
                        unit_of(2, tile_number(unit >> 1))

        @block.sync
        def _(sp):
            full = (CB - 1) * P * P
            for k, e in enumerate((src, dst, edge_type)):
                sp.dma_start(raw[:, k, 0:CB - 1, :],
                             e[0:full].rearrange("(g p e) -> p g e", g=CB - 1, p=P)).then_inc(raw_loaded[k], 16)
                sp.dma_start(raw[0:LAST, k, CB - 1, :],
                             e[full:full + LAST * P].rearrange("(p e) -> p e", p=LAST)).then_inc(raw_loaded[k], 16)
                if k == 1:
                    sp.dma_start(by_group[:, :], e.rearrange("(g e) -> g e", g=GROUPS)).then_inc(ends_loaded, 16)
            for n, ws in enumerate(sage_w):
                for m, w in enumerate(ws):
                    sp.dma_start(w_sage[:, n, m, :, :],
                                 w.rearrange("(k p) o -> p k o", p=P)).then_inc(sage_w_loaded, 16)
            for n, b in enumerate(sage_b):
                sp.dma_start(bias_sage[:, n, :], b.partition_broadcast(P)).then_inc(bias_loaded, 16)
            for n, b in enumerate(rel_b):
                sp.dma_start(bias_rel[:, n, :], b.partition_broadcast(P)).then_inc(bias_loaded, 16)

            def load_rel_w(n):
                for k in range(DK):
                    sp.dma_start(w_rel[:, n, k, :, :],
                                 rel_w[n][:, k * P:(k + 1) * P, :].rearrange("r p o -> p r o")
                                 ).then_inc(rel_w_loaded[n], 16)
            for n in range(LAYERS - SAGE):
                load_rel_w(n)

            def store_h(dram, n, k, t):
                sp.wait_ge(h_ready, n * TILES + k + 1)
                sp.dma_start(node_rows(dram, t), h_new[:, :]).then_inc(
                    out_stored if dram is out else h_stored, 16)

            def store_rels(n, k, t):
                for h in range(2):
                    sp.wait_ge(rel_relu, (n * TILES + k) * 2 + h + 1)
                    sp.dma_start(rel_dram[n][RH * h:RH * (h + 1), bass.ds(t * P, P), :]
                                 .rearrange("r p d -> p r d"), rel_out[:, h, :, :]).then_inc(rel_stored[h], 16)

            sp.dma_start(x_tile[:, :], node_rows(x, TILES - 1)).then_inc(x_loaded, 16)
            with sp.Fori(0, TILES - 1) as k:
                t = sp.snap(k * -1 + (TILES - 1))
                sp.wait_ge(x_turned, k + 1)
                sp.dma_start(x_tile[:, :], node_rows(x, t - 1)).then_inc(x_loaded, 16)
                store_h(h_dram[0], 0, k, t)
            store_h(h_dram[0], 0, TILES - 1, 0)

            for n in range(1, SAGE - 2):
                with sp.Fori(0, TILES) as k:
                    store_h(h_dram[n], n, k, sp.snap(k * -1 + (TILES - 1)))

            n = SAGE - 2
            def store_z(k, t):
                sp.wait_ge(z_kept, k + 1)
                sp.dma_start(node_rows(h_dram[n], t), z_new[:, :]).then_inc(h_stored, 16)
            sp.dma_start(x_res[:, :], node_rows(x, TILES - 1)).then_inc(res_loaded, 16)
            with sp.Fori(0, TILES - 1) as k:
                t = sp.snap(k * -1 + (TILES - 1))
                store_z(k, t)
                sp.wait_ge(res_used, k + 1)
                sp.dma_start(x_res[:, :], node_rows(x, t - 1)).then_inc(res_loaded, 16)
            store_z(TILES - 1, 0)

            n = SAGE - 1
            with sp.Fori(0, TILES) as k:
                t = sp.snap(k * -1 + (TILES - 1))
                store_h(x1_dram, n, k, t)
                store_rels(0, k, t)

            with sp.Fori(0, TILES) as k:
                store_rels(1, k, sp.snap(k * -1 + (TILES - 1)))

            sp.wait_ge(h_stored, 16 * (SAGE * TILES + 1))
            sp.wait_ge(res_used, TILES)
            sp.dma_start(x_res[:, :], node_rows(x1_dram, TILES - 1)).then_inc(res_loaded, 16)
            with sp.Fori(0, TILES - 1) as k:
                t = sp.snap(k * -1 + (TILES - 1))
                sp.wait_ge(res_used, TILES + k + 1)
                sp.dma_start(x_res[:, :], node_rows(x1_dram, t - 1)).then_inc(res_loaded, 16)
                store_h(out, SAGE, k, t)
            store_h(out, SAGE, TILES - 1, 0)
            sp.wait_ge(out_stored, 16 * (TILES + 1))
            for h in range(2):
                sp.wait_ge(rel_stored[h], 16 * (2 * TILES + 1))

        @block.gpsimd
        def _(pool):
            pool.memset(eps[:, :], EPS).then_inc(constants, 1)
            pool.memset(zeros[:, :], 0.0).then_inc(constants, 1)
            pool.wait_ge(constants, 2)
            pool.affine_select(out=ident[:, :], in_=zeros[:, 0:P], compare_op=ALU.not_equal, fill=1.0,
                               base=0, pattern=[[-1, P]], channel_multiplier=1).then_inc(identity_ready, 1)
            pool.affine_select(out=reverse[:, :], in_=zeros[:, 0:P], compare_op=ALU.not_equal, fill=1.0,
                               base=1 - GROUPS, pattern=[[1, P]], channel_multiplier=1).then_inc(constants, 1)
            pool.memset(ones[:, :], 1.0).then_inc(constants, 1)
            pool.memset(ring[:, :, :, D:DW], 1.0).then_inc(constants, 1)
            pool.iota(node_row[:, :], pattern=[[1, n_pad]], base=0, channel_multiplier=0,
                      allow_small_or_imprecise_dtypes=True).then_inc(constants, 1)

            for n in range(LAYERS):
                if 0 < n < SAGE:
                    pool.wait_ge(h_stored, 16 * (n * TILES + 1))
                elif n >= SAGE:
                    for h in range(2):
                        pool.wait_ge(rel_stored[h], 16 * ((n - SAGE + 1) * TILES + 1))
                with pool.Fori(0, ROUNDS) as i:
                    for s in range(SLOTS):
                        pool.wait_ge(idx_ready, n * GROUPS + SLOTS * i + s + 1)
                        wait_apart(pool)
                        for j in range(G):
                            pool.indirect_dma_start(
                                out=ring[:, s, j, 0:D], out_offset=None, in_=sources[n],
                                in_offset=bass.IndirectOffsetOnAxis(ap=idx[:, s, j:j + 1], axis=0),
                            ).then_inc(landed[s][j], 16)

        @block.scalar
        def _(act):
            def indices(n, g, s):
                cols = src_cols if n < SAGE else rel_cols
                act.activation(idx[:, s, :], group_cols(cols, g), ACT.Copy).then_inc(idx_ready, 1)

            def keep_turned(n, k):
                act.wait_ge(tile_turned, n * TILES + k + 1)
                if 0 < n < SAGE - 1:
                    act.wait_ge(right_ready, n * TILES + k)
                if n == SAGE - 1:
                    act.wait_ge(right_ready, n * TILES)
                act.activation(turned[:, :], ps_tail, ACT.Copy).then_inc(tile_kept, 1)

            def clear_tile(t):
                act.activation(tile_of(acc, t, DW), zeros[:, :], ACT.Copy).then_inc(cleared, 1)

            def tail(n, kind, k, over):
                t = None if k is None else k * -1 + (TILES - 1)
                if kind == 1 and n <= SAGE and n != SAGE - 1:
                    act.wait_ge(group_over, n * GROUPS + over)
                    act.activation(entry[:, :], tile_of(acc, t, D), ACT.Copy).then_inc(copied, 1)
                if kind == 1 and n == 0:
                    act.wait_ge(x_turned, k + 1)
                    act.activation(xT[:, :], ps_x, ACT.Copy).then_inc(x_kept, 1)
                if kind == 1 and n < SAGE - 1:
                    act.wait_ge(sums_turned, n * TILES + k + 1)
                    act.activation(sumsT[:, :], ps_tail, ACT.Copy).then_inc(sums_kept, 1)
                    if n == 0:
                        act.wait_ge(deg_ready, k + 1)
                        wait_apart(act)
                    clear_tile(t)
                    act.wait_ge(biased, n * TILES + k + 1)
                    act.activation(h_new[:, :], h_new[:, :], ACT.Relu).then_inc(h_ready, 1)
                if kind == 1 and n in (SAGE - 1, LAYERS - 1):
                    act.wait_ge(aggregated, (n // SAGE) * TILES + k + 1)
                    act.activation(std[:, 0:1], mv[:, 1:2], ACT.Sqrt, bias=eps[:, :]).then_inc(std_ready, 1)
                if kind == 1 and n == SAGE - 1:
                    clear_tile(t)
                if kind == 1 and n == SAGE or kind == 2 and n < SAGE:
                    keep_turned(n, k)
                if kind == 2 and n == SAGE - 1:
                    for h in range(2):
                        act.wait_ge(rel_biased, (k + 1) * QN + (h + 1) * QN // 2)
                        act.activation(rel_out[:, h, :, :], rel_out[:, h, :, :], ACT.Relu).then_inc(rel_relu, 1)
                if kind == 2 and n == SAGE - 2:
                    act.wait_ge(h_stored, 16 * (n * TILES + k + 1))
                    act.wait_ge(z_ready, k + 1)
                    act.activation(z_new[:, :], ps_x, ACT.Copy).then_inc(z_kept, 1)
                if kind == 1 and n == SAGE:
                    clear_tile(t)

            act.wait_ge(constants, 2)
            act.activation(first_root[:, :], eps[:, :], ACT.Sqrt)
            act.wait_ge(src_ready, 1)
            for n in range(LAYERS):
                if n > 0:
                    act.wait_ge(group_over, n * GROUPS)
                if n == SAGE:
                    act.wait_ge(rel_cols_ready, 1)
                for s in range(SLOTS):
                    indices(n, s, s)
                if n == 0:
                    act.activation(acc[:, :, :],
                                   zeros[:, :].rearrange("p (a d) -> p a d", a=1).to_broadcast([P, TILES, DW]),
                                   ACT.Copy).then_inc(cleared, 1)
                    act.wait_ge(words_ready, 1)

                def group(g, s, i, kind, k, word, n=n):
                    if not isinstance(g, int) or 1 <= g <= GROUPS - SLOTS:
                        act.wait_ge(group_over, n * GROUPS + g)
                        indices(n, g - 1 + SLOTS, (s - 1) % SLOTS)
                    tail(n, kind, k, g)
                layer_groups(act, group, False, n < LAYERS - 1)
                taken = act.value_load(counts[0:1, 0:1], min_val=0, max_val=2 * TILES - 2)
                units_left(act, taken, lambda kind, k, n=n: tail(n, kind, k, GROUPS), n < LAYERS - 1)

        @block.tensor
        def _(pe):
            def turn(target, source):
                for d in range(DK):
                    last = pe.transpose(target[:, d * P:(d + 1) * P], source[:, d * P:(d + 1) * P], ident[:, :])
                return last

            def multiply(target, source, w, start=True, stop=True):
                for d in range(DK):
                    last = pe.matmul(target, source[:, d * P:(d + 1) * P], w[d],
                                     start=start and d == 0, stop=stop and d == DK - 1)
                return last

            def sage_weights(n, m):
                return [w_sage[:, n, m, d, :] for d in range(DK)]

            def rel_product(m, k, q):
                before = max(p for p in range(-QN, q) if rel_bank[p % QN] == rel_bank[q])
                pe.wait_ge(rel_biased, (m * TILES + k + 1) * QN + before + 1)
                multiply(ps[:, rel_bank[q], :], turned,
                         [w_rel[:, m, d, q * QR:(q + 1) * QR, :].rearrange("p r o -> p (r o)")
                          for d in range(DK)]).then_inc(rel_ready, 1)

            def turn_new(n, k):
                pe.wait_ge(h_ready, n * TILES + k + 1)
                turn(ps_tail, h_new).then_inc(tile_turned, 1)

            def tail(n, kind, k, j):
                if kind == 1 and n == 0:
                    if j == 0:
                        pe.wait_ge(x_loaded, 16 * (k + 1))
                        pe.wait_ge(right_kept, 2 * k + 1)
                        turn(ps_x, x_tile).then_inc(x_turned, 1)
                    if j == ALL:
                        pe.wait_ge(x_kept, k + 1)
                        multiply(ps_x, xT, sage_weights(0, 1)).then_inc(x_right_ready, 1)
                if kind == 1 and n < SAGE - 1:
                    if j == 2:
                        pe.wait_ge(right_kept, 2 * k + 1 if n == 0 else (n + 1) * TILES + k + 1)
                        pe.wait_ge(copied, n * TILES + k + 1)
                        turn(ps_tail, entry).then_inc(sums_turned, 1)
                    if j == END:
                        pe.wait_ge(sums_kept, n * TILES + k + 1)
                        multiply(ps_tail, sumsT, sage_weights(n, 0)).then_inc(y_ready, 1)
                if kind == 2 and n < SAGE - 1:
                    if j == 2:
                        turn_new(n, k)
                    if j == END:
                        pe.wait_ge(tile_kept, n * TILES + k + 1)
                        if n == SAGE - 2:
                            multiply(ps_x, turned, sage_weights(n + 1, 0)).then_inc(z_ready, 1)
                        multiply(ps_tail, turned, sage_weights(n + 1, 1)).then_inc(right_ready, 1)
                if kind == 2 and n == SAGE - 1:
                    if j == 2:
                        pe.wait_ge(right_kept, (n + 1) * TILES + 1)
                        turn_new(n, k)
                    if j == ALL:
                        pe.wait_ge(tile_kept, n * TILES + k + 1)
                        rel_product(0, k, 0)
                    if j == END:
                        for q in range(1, QN):
                            rel_product(0, k, q)
                if n == SAGE:
                    if kind == 1 and j == 2:
                        pe.wait_ge(copied, (n - 1) * TILES + k + 1)
                        turn(ps_tail, entry).then_inc(tile_turned, 1)
                    if kind == 1 and j == END:
                        pe.wait_ge(tile_kept, n * TILES + k + 1)
                        rel_product(1, k, 0)
                        rel_product(1, k, 1)
                    if kind == 2 and j in (0, END):
                        rel_product(1, k, 3 if j == END else 2)

            pe.wait_ge(identity_ready, 1)
            for k in range(3):
                pe.wait_ge(raw_floated, k + 1)
                for b in range(CB):
                    n = LAST if b == CB - 1 else P
                    last = pe.transpose(ps[:, k, b * P:b * P + n], raw_f[0:n, k, b, :], ident[0:n, 0:n])
                last.then_inc(cols_turned, 1)
                if k == 1:
                    pe.wait_ge(constants, 6)
                    pe.wait_ge(ends_found, 1)
                    for e in range(3):
                        last = pe.matmul(ps_ends[:, e, :], ends[:, e:e + 1], reverse[0:GROUPS, 0:GROUPS],
                                         start=True, stop=True)
                    last.then_inc(ends_reversed, 1)
            pe.wait_ge(words_ready, 1)
            pe.wait_ge(rel_cols_ready, 1)

            for n in range(LAYERS):
                if n in (SAGE - 1, SAGE):
                    pe.wait_ge(rel_w_loaded[n - SAGE + 1], 16 * DK)
                if n == 0:
                    pe.wait_ge(sage_w_loaded, 16 * 2 * SAGE)

                def group(g, s, i, kind, k, word, n=n):
                    h = s % 2
                    span_word = load_word(pe, 0, g, 24)
                    before, extra = span_word >> (2 * TB + NB), bits_of(span_word, NB, TB)
                    needed = bits_of(span_word, 0, NB)
                    pe.wait_ge(first_marked, n * GROUPS + g + 1)
                    if n > 0 or not isinstance(g, int) or g >= 2:
                        pe.wait_ge(group_over, n * GROUPS + g - 1)

                    def product(j, start=False, stop=False):
                        pe.wait_ge(landed[s][j], 16 * (n * ROUNDS + i + 1))
                        return pe.matmul(ps[:, h, 0:DW], onehot[:, h, j, :], ring[:, s, j, :],
                                         start=start, stop=stop)
                    for j in range(LEAD, G - 1):
                        product(j, start=j == LEAD)
                        tail(n, kind, k, j - LEAD)
                    with pe.If(needed > 3):
                        product(G - 1)
                        for j in range(LEAD):
                            last = product(j, stop=j == LEAD - 1)
                        last.then_inc(first_summed, 1)
                    with pe.If(needed < 4):
                        for j in range(LEAD):
                            pe.wait_ge(landed[s][j], 16 * (n * ROUNDS + i + 1))
                        product(G - 1, stop=True).then_inc(first_summed, 1)
                    tail(n, kind, k, ALL)
                    with pe.If(extra > 0):
                        with pe.Fori(before + 1, before + extra + 1) as number:
                            pe.wait_ge(extra_marked[n], number)

                            def products(count):
                                for j in range(count):
                                    last = pe.matmul(ps[:, EXTRA, 0:DW], onehot[:, EXTRA, j, :], ring[:, s, j, :],
                                                     start=(j == 0), stop=(j == count - 1))
                                last.then_inc(extra_summed[n], 1)
                            for code, count in enumerate(COUNTS):
                                with pe.If((needed & 3) == code):
                                    products(count)
                    tail(n, kind, k, END)
                layer_groups(pe, group, False, n < LAYERS - 1)
                if n < LAYERS - 1:
                    taken = pe.value_load(counts[0:1, 0:1], min_val=0, max_val=2 * TILES - 2)

                    def unit(kind, k, n=n):
                        for j in (*range(G), ALL, END):
                            tail(n, kind, k, j)
                    units_left(pe, taken, unit, True)

        @block.vector
        def _(dve):
            linked = [0]

            def link(ins):
                linked[0] += 1
                ins.then_inc(dve_link, 1)
                dve.wait_ge(dve_link, linked[0])

            dve.sem_inc(rel_biased, QN)
            dve.sem_inc(right_kept, 1)
            for ahead in (h_stored, *rel_stored, out_stored):
                dve.sem_inc(ahead, 16)

            for k in range(3):
                dve.wait_ge(raw_loaded[k], 32)
                dve.tensor_copy(raw_f[:, k, 0:CB - 1, :], raw[:, k, 0:CB - 1, :])
                dve.tensor_copy(raw_f[0:LAST, k, CB - 1, :], raw[0:LAST, k, CB - 1, :]).then_inc(raw_floated, 1)
                if k == 1:
                    dve.wait_ge(cols_turned, 1)
                    dve.tensor_copy(src_cols[:, :], ps[:, 0, 0:CHUNKS]).then_inc(src_ready, 1)
            dve.wait_ge(cols_turned, 2)
            dve.tensor_copy(dst_cols[:, :], ps[:, 1, 0:CHUNKS]).then_inc(dst_ready, 1)
            dve.wait_ge(ends_loaded, 16)
            chunked = by_group[:, :].rearrange("g (c p) -> g c p", c=G)
            link(dve.tensor_reduce(by_chunk[:, 0, :], chunked, axis=AX.X, op=ALU.max))
            link(dve.tensor_reduce(by_chunk[:, 1, :], chunked, axis=AX.X, op=ALU.min))
            link(dve.tensor_copy(by_chunk_i[:, :, :], by_chunk[:, :, :]))
            link(dve.tensor_scalar(by_chunk_i[:, :, :], by_chunk_i[:, :, :], P.bit_length() - 1, None,
                                   op0=ALU.arith_shift_right))
            link(dve.tensor_copy(by_chunk[:, :, :], by_chunk_i[:, :, :]))
            link(dve.tensor_reduce(ends[:, 0:1], by_chunk[:, 0, :], axis=AX.X, op=ALU.max))
            link(dve.tensor_reduce(ends[:, 1:2], by_chunk[:, 1, :], axis=AX.X, op=ALU.min))
            link(dve.tensor_reduce(needs[:, 0:1], by_chunk[:, 0, 0:LEAD], axis=AX.X, op=ALU.max))
            link(dve.tensor_reduce(needs[:, 1:2], by_chunk[:, 1, COUNTS[1]:G], axis=AX.X, op=ALU.min))
            link(dve.tensor_reduce(needs[:, 2:3], by_chunk[:, 1, COUNTS[0]:G], axis=AX.X, op=ALU.min))
            link(dve.tensor_tensor(needs[:, 0:1], needs[:, 0:1], ends[:, 0:1], op=ALU.is_ge))
            link(dve.tensor_tensor(needs[:, 1:3], needs[:, 1:3], ends[:, 0:1].to_broadcast([GROUPS, 2]),
                                   op=ALU.is_lt))
            link(dve.scalar_tensor_tensor(needs[:, 0:1], needs[:, 0:1], 2.0, needs[:, 1:2],
                                          op0=ALU.mult, op1=ALU.add))
            dve.scalar_tensor_tensor(ends[:, 2:3], needs[:, 0:1], 2.0, needs[:, 2:3],
                                     op0=ALU.mult, op1=ALU.add).then_inc(ends_found, 1)

            (high, extra, through, before, word, avail, taken_by, change, shifted, other, unit_row, low, needed) = (
                plan[0:1, n, :] for n in range(13))
            link(dve.memset(plan[:, :, :], 0.0))
            dve.wait_ge(ends_reversed, 1)
            link(dve.tensor_copy(high[:, 0:GROUPS], ps_ends[:, 0, :]))
            link(dve.tensor_copy(low[:, 0:GROUPS], ps_ends[:, 1, :]))
            link(dve.tensor_copy(needed[:, 0:GROUPS], ps_ends[:, 2, :]))
            dve.wait_ge(constants, 6)
            link(dve.tensor_tensor(extra[:, 0:GROUPS], high[:, 0:GROUPS], low[:, 0:GROUPS], op=ALU.subtract))
            link(dve.tensor_tensor_scan(through[:, 0:GROUPS], extra[:, 0:GROUPS], zeros[0:1, 0:GROUPS], 0.0,
                                        op0=ALU.add, op1=ALU.add))
            link(dve.tensor_tensor(before[:, 0:GROUPS], through[:, 0:GROUPS], extra[:, 0:GROUPS], op=ALU.subtract))
            link(dve.scalar_tensor_tensor(word[:, 0:GROUPS], before[:, 0:GROUPS], float(1 << TB), high[:, 0:GROUPS],
                                          op0=ALU.mult, op1=ALU.add))
            link(dve.scalar_tensor_tensor(word[:, 0:GROUPS], word[:, 0:GROUPS], float(1 << TB), extra[:, 0:GROUPS],
                                          op0=ALU.mult, op1=ALU.add))
            link(dve.scalar_tensor_tensor(words[0:1, 0, :], word[:, 0:GROUPS], float(1 << NB), needed[:, 0:GROUPS],
                                          op0=ALU.mult, op1=ALU.add))
            link(dve.tensor_copy(shifted[:, 0:GROUPS], high[:, 0:GROUPS]))
            rows, step = [shifted, other], 1
            while step < GROUPS:
                link(dve.tensor_tensor(rows[1][:, 0:GROUPS], rows[0][:, 0:GROUPS], rows[0][:, step:step + GROUPS],
                                       op=ALU.max))
                rows, step = rows[::-1], 2 * step
            link(dve.tensor_scalar(avail[:, 2:GROUPS], rows[0][:, 2:GROUPS], -2.0, 2.0 * (TILES - 1),
                                   op0=ALU.mult, op1=ALU.add))
            link(dve.tensor_tensor_scan(taken_by[:, 1:GROUPS + 1], ones[0:1, 0:GROUPS], avail[:, 0:GROUPS], 0.0,
                                        op0=ALU.add, op1=ALU.min))
            link(dve.tensor_copy(counts[0:1, 0:1], taken_by[:, GROUPS:GROUPS + 1]))
            link(dve.tensor_tensor(change[:, 0:GROUPS], taken_by[:, 1:GROUPS + 1], taken_by[:, 0:GROUPS],
                                   op=ALU.subtract))
            unit_i, tile_i, second_i = (plan_i[0:1, n, :] for n in range(3))
            link(dve.tensor_copy(unit_i, taken_by[:, 0:GROUPS]))
            link(dve.tensor_scalar(tile_i, unit_i, 1, None, op0=ALU.arith_shift_right))
            link(dve.tensor_scalar(second_i, unit_i, 1, None, op0=ALU.bitwise_and))
            link(dve.scalar_tensor_tensor(unit_row[:, 0:GROUPS], tile_i, float(1 << KB), second_i,
                                          op0=ALU.mult, op1=ALU.add))
            link(dve.scalar_tensor_tensor(unit_row[:, 0:GROUPS], unit_row[:, 0:GROUPS], 1.0, change[:, 0:GROUPS],
                                          op0=ALU.add, op1=ALU.mult))
            link(dve.scalar_tensor_tensor(unit_row[:, 0:GROUPS], high[:, 2:GROUPS + 2], float(1 << KB + TB),
                                          unit_row[:, 0:GROUPS], op0=ALU.mult, op1=ALU.add))
            link(dve.tensor_scalar(extra[:, 0:GROUPS], extra[:, 0:GROUPS], 1.0, float(1 << KB + 2 * TB),
                                   op0=ALU.min, op1=ALU.mult))
            link(dve.tensor_tensor(unit_row[:, 0:GROUPS], extra[:, 1:GROUPS + 1], unit_row[:, 0:GROUPS], op=ALU.add))
            link(dve.scalar_tensor_tensor(unit_row[:, 0:GROUPS], high[:, 1:GROUPS + 1],
                                          float(1 << KB + 2 * TB + 1), unit_row[:, 0:GROUPS],
                                          op0=ALU.mult, op1=ALU.add))
            link(dve.scalar_tensor_tensor(words[0:1, 1, :], high[:, 0:GROUPS], float(1 << KB + 3 * TB + 1),
                                          unit_row[:, 0:GROUPS], op0=ALU.mult, op1=ALU.add))
            dve.sem_inc(words_ready, 1)

            dve.wait_ge(cols_turned, 3)
            dve.scalar_tensor_tensor(rel_cols[:, :], ps[:, 2, 0:CHUNKS], float(n_pad), src_cols[:, :],
                                     op0=ALU.mult, op1=ALU.add).then_inc(rel_cols_ready, 1)
            dve.wait_ge(bias_loaded, 16 * LAYERS)

            def mark(buffer, g, t):
                return dve.tensor_tensor(
                    onehot[:, buffer, :, :],
                    node_row[:, bass.ds(t * P, P)].rearrange("p (a d) -> p a d", a=1).to_broadcast([P, G, P]),
                    group_cols(dst_cols, g).rearrange("p (g a) -> p g a", a=1).to_broadcast([P, G, P]),
                    op=ALU.is_equal)

            def mark_extra(n, g, t):
                mark(EXTRA, g, tile_number(t)).then_inc(extra_marked[n], 1)

            def add(n, bank, t):
                dve.tensor_tensor(tile_of(acc, t, DW), tile_of(acc, t, DW), ps[:, bank, 0:DW],
                                  op=ALU.add).then_inc(added[n], 1)

            def bias_rel_product(m, k, q):
                dve.wait_ge(rel_ready, (m * TILES + k) * QN + q + 1)
                if q % (QN // 2) == 0:
                    dve.wait_ge(rel_stored[2 * q // QN], 16 * (m * TILES + k + 1))
                part = rel_out[:, q * QR // RH, q * QR % RH:q * QR % RH + QR, :]
                dve.tensor_tensor(part, ps[:, rel_bank[q], :].rearrange("p (r d) -> p r d", r=QR),
                                  bias_rel[:, m:m + 1, :].to_broadcast([P, QR, D]),
                                  op=ALU.add).then_inc(rel_biased, 1)
                if m == 1 and q % (QN // 2) == QN // 2 - 1:
                    half = rel_out[:, 2 * q // QN, :, :]
                    dve.wait_ge(rel_biased, (m * TILES + k + 1) * QN + q + 1)
                    dve.tensor_scalar(half, half, 0.0, None, op0=ALU.max).then_inc(rel_relu, 1)

            def layer_norm(m, k):
                done = m * TILES + k + 1
                dve.bn_stats(stats[:, :], h_new[:, :]).then_inc(stats_ready, 1)
                dve.wait_ge(stats_ready, done)
                wait_apart(dve)
                dve.bn_aggr(mv[:, :], stats[:, :]).then_inc(aggregated, 1)
                dve.wait_ge(std_ready, done)
                dve.reciprocal(std[:, 1:2], std[:, 0:1]).then_inc(inverse_ready, 1)
                dve.wait_ge(inverse_ready, done)
                dve.tensor_scalar(h_new[:, :], h_new[:, :], mv[:, 0:1], std[:, 1:2],
                                  op0=ALU.subtract, op1=ALU.mult).then_inc(h_ready, 1)

            def tail(n, kind, k, over):
                t = None if k is None else k * -1 + (TILES - 1)
                if kind == 1 and n == 0:
                    factor = rdeg[:, bass.ds(t, 1)]
                    dve.wait_ge(group_over, over)
                    dve.tensor_scalar(factor, acc[:, bass.ds(t, 1), D:DW].rearrange("p a d -> p (a d)"), 1.0, None,
                                      op0=ALU.max).then_inc(deg_clamped, 1)
                    dve.wait_ge(deg_clamped, k + 1)
                    wait_apart(dve)
                    dve.reciprocal(factor, factor).then_inc(deg_ready, 1)
                    dve.wait_ge(x_right_ready, k + 1)
                    dve.tensor_tensor(tile_of(right, t, D), ps_x, bias_sage[:, 0, :],
                                      op=ALU.add).then_inc(right_kept, 1)
                if kind == 1 and n < SAGE:
                    dve.wait_ge(h_stored, 16 * (n * TILES + (0 if n == SAGE - 2 else k) + 1))
                    if n == 0:
                        dve.wait_ge(deg_ready, k + 1)
                        dve.wait_ge(right_kept, 2 * k + 2)
                    if n < SAGE - 1:
                        dve.wait_ge(y_ready, n * TILES + k + 1)
                    else:
                        dve.wait_ge(group_over, n * GROUPS + over)
                        dve.wait_ge(tile_turned, n * TILES + k)
                        wait_apart(dve)
                    dve.scalar_tensor_tensor(h_new[:, :], ps_tail if n < SAGE - 1 else tile_of(acc, t, D),
                                             rdeg[:, bass.ds(t, 1)], tile_of(right, t, D),
                                             op0=ALU.mult, op1=ALU.add).then_inc(biased, 1)
                    if n == SAGE - 1:
                        dve.wait_ge(biased, n * TILES + k + 1)
                        wait_apart(dve)
                        layer_norm(0, k)
                if kind == 2 and n < SAGE - 1:
                    if n == SAGE - 2:
                        dve.wait_ge(res_loaded, 16 * (k + 1))
                        dve.tensor_tensor(x_res[:, :], x_res[:, :], bias_sage[:, n + 1, :],
                                          op=ALU.add).then_inc(res_biased, 1)
                        dve.wait_ge(res_biased, k + 1)
                    dve.wait_ge(right_ready, n * TILES + k + 1)
                    kept = dve.tensor_tensor(tile_of(right, t, D), ps_tail,
                                             x_res[:, :] if n == SAGE - 2 else bias_sage[:, n + 1, :], op=ALU.add)
                    kept.then_inc(right_kept, 1)
                    if n == SAGE - 2:
                        dve.wait_ge(right_kept, TILES + n * TILES + k + 2)
                        dve.sem_inc(res_used, 1)
                if kind == 2 and n == SAGE - 1:
                    for q in range(QN):
                        bias_rel_product(0, k, q)
                if n == SAGE:
                    for q in ([], [0, 1], range(2, QN))[kind]:
                        bias_rel_product(1, k, q)
                if n == LAYERS - 1 and kind == 1:
                    dve.wait_ge(group_over, n * GROUPS + over)
                    dve.wait_ge(res_loaded, 16 * (TILES + k + 1))
                    dve.wait_ge(out_stored, 16 * (k + 1))
                    dve.tensor_tensor(h_new[:, :], tile_of(acc, t, D), x_res[:, :], op=ALU.add).then_inc(res_used, 1)
                    dve.wait_ge(res_used, TILES + k + 1)
                    wait_apart(dve)
                    layer_norm(1, k)

            for n in range(LAYERS):
                span_word = load_word(dve, 0, 0, 24)
                high = bits_of(span_word, NB + TB, TB)
                mark(0, 0, tile_number(high)).then_inc(first_marked, 1)
                mark(1, 1, tile_number(bits_of(load_word(dve, 1, 0, WORD_BITS), KB + 2 * TB + 1, TB))).then_inc(first_marked, 1)
                with dve.If(bits_of(span_word, NB, TB) > 0):
                    mark_extra(n, 0, high - 1)
                dve.wait_ge(cleared, n * TILES + 1)
                if n == LAYERS - 1:
                    dve.wait_ge(h_stored, 16 * (SAGE * TILES + 1))

                def group(g, s, i, kind, k, word, n=n):
                    h = s % 2
                    high = tile_number(word >> (KB + 3 * TB + 1))
                    alone = kind == 1 and n in (SAGE - 1, LAYERS - 1)
                    if alone:
                        tail(n, kind, k, g)
                    dve.wait_ge(first_summed, n * GROUPS + g + 1)
                    add(n, h, high)
                    span_word = load_word(dve, 0, g, 24)
                    before, extra = span_word >> (2 * TB + NB), bits_of(span_word, NB, TB)
                    with dve.If(extra > 0):
                        dve.wait_ge(extra_summed[n], before + 1)
                        dve.wait_ge(added[n], before + g + 1)
                        add(n, EXTRA, tile_number(high - 1))
                        with dve.If(extra > 1):
                            with dve.Fori(before + 2, before + extra + 1) as number:
                                t = high + before - number
                                mark_extra(n, g, t)
                                dve.wait_ge(extra_summed[n], number)
                                dve.wait_ge(added[n], number + g)
                                add(n, EXTRA, tile_number(t))
                    dve.wait_ge(added[n], before + extra + g + 1)
                    dve.sem_inc(group_over, 1)

                    if n < SAGE - 1:
                        tail(n, kind, k, g)
                    if not (isinstance(g, int) and g == GROUPS - 1):
                        with dve.If(bits_of(word, KB + 2 * TB, 1) > 0):
                            mark_extra(n, g + 1, bits_of(word, KB + 2 * TB + 1, TB) - 1)
                    if not (isinstance(g, int) and g >= GROUPS - 2):
                        mark(h, g + 2, tile_number(bits_of(word, KB + TB, TB))).then_inc(first_marked, 1)
                    if not alone and n >= SAGE - 1:
                        tail(n, kind, k, g)
                layer_groups(dve, group, True, n < LAYERS - 1)
                taken = dve.value_load(counts[0:1, 0:1], min_val=0, max_val=2 * TILES - 2)

                def unit(kind, k, n=n):
                    tail(n, kind, k, GROUPS)
                units_left(dve, taken, unit, n < LAYERS - 1)


def kernel(**inputs):
    import numpy as np
    import concourse.bacc as bacc
    from concourse.bass_utils import run_bass_kernel_spmd

    x = np.asarray(inputs["x"])
    n_nodes, d = x.shape
    n_edges = inputs["src"].shape[0]
    w_rel = [np.ascontiguousarray(inputs[f"L1_gnn_W{n}"]) for n in range(2)]
    n_rel = w_rel[0].shape[0]
    added_nodes, added_edges = P - n_nodes % P, -n_edges % (SLOTS * G * P)
    arrays = {
        "x": np.pad(x, ((0, added_nodes), (0, 0))),
        "src": np.pad(np.asarray(inputs["src"]), (0, added_edges), mode="edge"),
        "dst": np.pad(np.asarray(inputs["dst"]), (0, added_edges), constant_values=n_nodes + added_nodes - 1),
        "edge_type_8": np.pad(np.asarray(inputs["edge_type_8"]), (0, added_edges), mode="edge"),
        **{f"W{n}{s}": np.ascontiguousarray(np.asarray(inputs[f"L0_gnn_W{n}{s}"]).T) for n in (1, 2, 3) for s in "lr"},
        **{f"b{n}": np.asarray(inputs[f"L0_gnn_b{n}l"]) for n in (1, 2, 3)},
        **{f"Wrel{n}": w_rel[n] for n in range(2)},
        **{f"brel{n}": np.asarray(inputs[f"L1_gnn_b{n}"]) for n in range(2)},
    }
    nc = bacc.Bacc("TRN2", target_bir_lowering=False, num_devices=1)
    t = {k: nc.dram_tensor(f"in_{k}", a.shape, mybir.dt.from_np(a.dtype), kind="ExternalInput").ap()
         for k, a in arrays.items()}
    out = nc.dram_tensor("out", arrays["x"].shape, mybir.dt.float32, kind="ExternalOutput").ap()
    build(nc, t["x"], t["src"], t["dst"], t["edge_type_8"],
          [(t[f"W{n}l"], t[f"W{n}r"]) for n in (1, 2, 3)], [t[f"b{n}"] for n in (1, 2, 3)],
          [t["Wrel0"], t["Wrel1"]], [t["brel0"], t["brel1"]], out, n_rel)
    r = run_bass_kernel_spmd(nc, [{f"in_{k}": a for k, a in arrays.items()}], core_ids=[0])
    return r.results[0]["out"][:n_nodes]
```
